# Optimizing a Trainium2 kernel written in Bass

```python
import numpy as np
import jax
import jax.numpy as jnp

def _softmax(x, axis=-1):
    return jax.nn.softmax(x, axis=axis)

def _gelu(x):
    return jax.nn.gelu(x, approximate=True)

def _silu(x):
    return jax.nn.silu(x)

def _sigmoid(x):
    return jax.nn.sigmoid(x)

def _layernorm(x, axis=-1, eps=1e-05):
    m = jnp.mean(x, axis=axis, keepdims=True)
    v = jnp.var(x, axis=axis, keepdims=True)
    return (x - m) / jnp.sqrt(v + eps)

def _scatter_add(tgt, idx, src, axis=0):
    return tgt.at[idx].add(src)

def _segment_sum(src, seg, n):
    return jax.ops.segment_sum(src, seg, n)
kernel_name = 'mk_adj_preln_d2_adj_r2_8cb5dd'

def setup_inputs(seed: int=0):
    np.random.seed(seed)
    _w = jnp.asarray

    def _rec_inputs():
        import jax
        import jax.numpy as jnp
        _gk = jax.random.key(seed)
        x = -9.806e-05 + 1 * jax.random.normal(jax.random.fold_in(_gk, 1), (4096, 64), jnp.float32)
        _a = jax.random.bernoulli(jax.random.fold_in(_gk, 2), 0.00390625, (4096, 4096))
        _a = jnp.logical_or(_a, jnp.swapaxes(_a, -1, -2))
        _a = jnp.logical_or(_a, jnp.eye(4096, dtype=bool))
        adj = _a.astype(jnp.int32)
        return (x, adj)
    x, adj = _rec_inputs()

    def _L0_gnn_setup():
        import jax, jax.numpy as jnp
        import numpy as np
        ALPHA = 0.2
        NEG_BIG = -9000000000000000.0
        key = jax.random.key(seed)
        k1, k2, k3, k4, k5 = jax.random.split(key, 5)
        N, M, F_in, F_out = (4096, 4096, 64, 64)
        item_embs = jax.random.normal(k1, (N, F_in), dtype=jnp.float32)
        entity_embs = jax.random.normal(k2, (M, F_in), dtype=jnp.float32)
        adj = jax.random.randint(k3, (N, M), 0, 2, dtype=jnp.int32)
        W = jax.random.normal(k4, (F_in, F_out), dtype=jnp.float32)
        a = jax.random.normal(k5, (2 * F_out, 1), dtype=jnp.float32)
        return {'item_embs': item_embs, 'entity_embs': entity_embs, 'adj': adj, 'W': W, 'a': a}
    _L0_gnn_all = _L0_gnn_setup()
    _L0_gnn_in = {k: v for k, v in _L0_gnn_all.items() if k in ('entity_embs', 'W', 'a')}
    del _L0_gnn_all

    def _L1_gnn_setup():
        import jax, jax.numpy as jnp
        import numpy as np
        N = 8192
        D = 64
        key = jax.random.key(seed)
        k1, k2, k3 = jax.random.split(key, 3)
        x = jax.random.normal(k1, (N, D), dtype=jnp.float32)
        adj_mat = jax.random.randint(k2, (N, N), 0, 2, dtype=jnp.int32)
        U = jax.random.normal(k3, (D, D), dtype=jnp.float32)
        return {'x': x, 'adj_mat': adj_mat, 'U': U}
    _L1_gnn_all = _L1_gnn_setup()
    _L1_gnn_in = {k: v for k, v in _L1_gnn_all.items() if k in ('U',)}
    del _L1_gnn_all
    return {'x': x, 'adj': adj, 'L0_gnn_entity_embs': _L0_gnn_in['entity_embs'], 'L0_gnn_W': _L0_gnn_in['W'], 'L0_gnn_a': _L0_gnn_in['a'], 'L1_gnn_U': _L1_gnn_in['U']}

def reference(x, adj, L0_gnn_entity_embs, L0_gnn_W, L0_gnn_a, L1_gnn_U):
    import jax
    import jax.numpy as jnp

    def _L0_gnn_ref(item_embs, entity_embs, adj, W, a):
        import jax, jax.numpy as jnp
        import numpy as np
        ALPHA = 0.2
        NEG_BIG = -9000000000000000.0
        F_out = W.shape[1]
        Wh = item_embs @ W
        We = entity_embs @ W
        a1 = a[:F_out, 0]
        a2 = a[F_out:, 0]
        scores = (Wh @ a1)[:, None] + (We @ a2)[None, :]
        e = jnp.where(scores > 0, scores, ALPHA * scores)
        e = jnp.where(adj > 0, e, NEG_BIG)
        attention = jax.nn.softmax(e, axis=1)
        entity_emb_weighted = attention @ entity_embs
        h_prime = entity_emb_weighted + item_embs
        return jax.nn.elu(h_prime)

    def _L1_gnn_ref(x, adj_mat, U):
        import jax, jax.numpy as jnp
        import numpy as np
        N = 8192
        D = 64
        a = adj_mat.astype(x.dtype)
        deg = a.sum(axis=0)
        agg = jnp.einsum('ji,jd->id', a, x)
        out = jax.nn.relu(agg @ U.T / deg[:, None])
        return out
    h = jnp.maximum(_layernorm(x, axis=-1), 0.0)
    x = x + _L0_gnn_ref(h, L0_gnn_entity_embs, adj, L0_gnn_W, L0_gnn_a)
    h = jnp.maximum(_layernorm(x, axis=-1), 0.0)
    x = x + _L1_gnn_ref(h, adj, L1_gnn_U)
    return x

_drawn_inputs = setup_inputs


def setup_inputs(seed=0):
    import zlib

    import numpy as np

    out = dict(_drawn_inputs(seed))
    spreads = {}
    factors = {}
    for name, (base, spread) in spreads.items():
        noise = np.random.default_rng([zlib.crc32(name.encode()), seed]).standard_normal(out[name].shape)
        drawn = base * np.exp(spread * noise) if base else spread * noise
        out[name] = jnp.asarray(drawn.astype(out[name].dtype))
    for name, factor in factors.items():
        out[name] = (out[name] * factor).astype(out[name].dtype)
    return out
```

```python
from contextlib import ExitStack

import concourse.bass as bass
from concourse import mybir



def graph_layers_kernel(nc: bass.Bass, x, adj, V, W, a, U, out):
    fp32, fp16, bf16 = mybir.dt.float32, mybir.dt.float16, mybir.dt.bfloat16
    ALU = mybir.AluOpType
    ACT = mybir.ActivationFunctionType
    AX = mybir.AxisListType

    P = 128
    N, D = x.shape
    M = V.shape[0]
    NB = N // P
    NC = M // P
    G = 4
    NG = NC // G
    HALF = M // 2
    E = D + 1
    CB = 512 // E
    NSUM = -(-NB // CB)
    LAG = 3
    UNROLL = 6
    LOOPS = (NB - LAG) // UNROLL
    AHEAD = 2
    BODY = NB - AHEAD - LOOPS * UNROLL
    SLOPE = 0.2
    MASKED = -float(2 ** 53)
    EPS = 1e-5
    H2SCALE = 4096.0
    ADJ_SLOTS, W_SLOTS, R_SLOTS, PT_SLOTS, T_BANKS = 6, 3, 2, 4, 2
    RELU_AT, ELU_AT = (0, 2), 1
    STORES = 4
    LN1_VAR = 6

    adj_blocks = adj.rearrange("(k p) m -> p k m", p=P)
    x_view = x.rearrange("(k p) d -> p k d", p=P)
    v_view = V.rearrange("(c p) d -> p c d", p=P)
    out_view = out.rearrange("(k p) d -> p k d", p=P)

    ctx = ExitStack()
    with ctx:
        def sb(name, shape, dt=fp32):
            return ctx.enter_context(nc.sbuf_tensor(name, shape, dt))

        def sem(name):
            return ctx.enter_context(nc.semaphore(name))

        adj_ring = [sb(f"adj{i}", [P, M], bf16) for i in range(ADJ_SLOTS)]
        w = [sb(f"w{i}", [P, M]) for i in range(W_SLOTS)]
        r = [sb(f"r{i}", [P, M]) for i in range(R_SLOTS)]
        mask = sb("mask", [P, M], bf16)
        t_row = sb("t_row", [P, M])
        pt = sb("pt", [P, PT_SLOTS, G * P])
        ident = sb("ident", [P, P])
        x_sb = sb("x_sb", [P, NB, D])
        h1 = sb("h1", [P, NB, D])
        x1 = sb("x1", [P, NB, D])
        ve = sb("ve", [P, NC, E])
        vt = sb("vt", [D, 2, G * P])
        work = r[1][:, 0:NB * D].rearrange("p (k d) -> p k d", d=D)
        w_sb = sb("w_sb", [D, D])
        u_sb = sb("u_sb", [D, D])
        a_sb = sb("a_sb", [D, 2])
        a_rep = sb("a_rep", [D, 2, P])
        wt = sb("wt", [D, D])
        ut = sb("ut", [D, D])
        wa1_row = sb("wa1_row", [P, D])
        wa2_rep = sb("wa2_rep", [D, P])
        s_col = sb("s_col", [P, NB])
        s_low = sb("s_low", [P, NB])
        s_high = sb("s_high", [P, NB])
        mean1 = sb("mean1", [P, NB])
        var1 = sb("var1", [P, NB])
        root1 = sb("root1", [P, NB])
        rstd1 = sb("rstd1", [P, NB])
        tmp1 = sb("tmp1", [P, NB])
        w_max = sb("w_max", [P, 1])
        z_max = sb("z_max", [P, 1])
        m_col = sb("m_col", [P, 1])
        c_col = sb("c_col", [P, 2])
        rden = sb("rden", [P, 1])
        hp = sb("hp", [P, D])
        x1_now = sb("x1_now", [P, D])
        hp_low = sb("hp_low", [P, D])
        hp_exp = sb("hp_exp", [P, D])
        hp_pos = sb("hp_pos", [P, D])
        elu = sb("elu", [P, D])
        stats = sb("stats", [P, 6])
        mv = sb("mv", [P, 2])
        var_eps = sb("var_eps", [P, 1])
        rstd2 = sb("rstd2", [P, 2])
        minus_half = sb("minus_half", [P, 1])
        h2s = sb("h2s", [P, D])
        h2c = sb("h2c", [P, D])
        h2hi = sb("h2hi", [P, 2, E], fp16)
        h2lo = sb("h2lo", [P, 2, D], fp16)
        rdeg = sb("rdeg", [P, NB])
        agg = work
        aggt = sb("aggt", [D, 2, G * P])
        fin = h1

        sums = [ctx.enter_context(nc.psum_tensor(f"sums{i}", [P, 512], fp32)) for i in range(NSUM)]
        tb = [ctx.enter_context(nc.psum_tensor(f"tb{i}", [P, 512], fp32)) for i in range(T_BANKS)]
        att = ctx.enter_context(nc.psum_tensor("att", [P, 512], fp32))

        adj_in = [sem(f"adj_in{i}") for i in range(ADJ_SLOTS)]
        small_in, v_in, x_in, out_stored = sem("small_in"), sem("v_in"), sem("x_in"), sem("out_stored")
        consts = sem("consts")
        a_repeated = sem("a_repeated")
        wu_turned = sem("wu_turned")
        wu_copied = sem("wu_copied")
        wa_made = sem("wa_made")
        wa_copied = sem("wa_copied")
        v_turned = sem("v_turned")
        v_copied = sem("v_copied")
        t_made = sem("t_made")
        t_copied = sem("t_copied")
        ln1 = sem("ln1")
        root_done = sem("root_done")
        s_done = sem("s_done")
        mask_done = sem("mask_done")
        w_done = sem("w_done")
        z_done = sem("z_done")
        m_done = sem("m_done")
        c_done = sem("c_done")
        relu_z = sem("relu_z")
        lowered = sem("lowered")
        transposed = sem("transposed")
        weights = sem("weights")
        attended = sem("attended")
        rden_done = sem("rden_done")
        hp_done = sem("hp_done")
        low_done = sem("low_done")
        pos_done = sem("pos_done")
        exp_done = sem("exp_done")
        sum_done = sem("sum_done")
        elu_done = sem("elu_done")
        x1_done = sem("x1_done")
        x1_kept = sem("x1_kept")
        stats_done = sem("stats_done")
        mv_done = sem("mv_done")
        eps_done = sem("eps_done")
        pow_done = sem("pow_done")
        rstd_done = sem("rstd_done")
        norm_done = sem("norm_done")
        relu_done = sem("relu_done")
        hi_done = sem("hi_done")
        lo_done = sem("lo_done")
        gathered = sem("gathered")
        rdeg_done = sem("rdeg_done")
        agg_done = sem("agg_done")
        agg_turned = sem("agg_turned")
        aggt_copied = sem("aggt_copied")
        product_done = sem("product_done")
        fin_done = sem("fin_done")

        block = ctx.enter_context(nc.Block())

        def run_steps(engine, step):
            for k in range(BODY):
                step(k, k, 0)
            with engine.Fori(0, LOOPS) as it:
                for u in range(UNROLL):
                    step(it * UNROLL + (BODY + u), BODY + u, it)
            for k in range(BODY + LOOPS * UNROLL, NB + LAG):
                step(k, k, 0)

        def wait_all(engine, ready, *pairs):
            for _, value in pairs:
                if not isinstance(value, int):
                    engine.compute_val(value)
            engine.wait_ge(*ready)
            for semaphore, value in pairs:
                engine.wait_ge(semaphore, value)

        def live(s, lag):
            return lag <= s < NB + lag

        def at(tensor, q):
            return tensor[:, bass.ds(q, 1), :].rearrange("p o d -> p (o d)")

        @block.sync
        def _(sp):
            sp.dma_start(w_sb[:, :], W[:, :]).then_inc(small_in, 16)
            sp.dma_start(u_sb[:, :], U[:, :]).then_inc(small_in, 16)
            with nc.allow_non_contiguous_dma(reason="2 x 64 numbers"):
                sp.dma_start(a_sb[:, :], a.rearrange("(h d) o -> d (h o)", h=2)).then_inc(small_in, 16)
            sp.dma_start(ve[:, :, 0:D], v_view).then_inc(v_in, 16)
            sp.dma_start(x_sb[:, :, :], x_view).then_inc(x_in, 16)
            for i in range(STORES):
                sp.wait_ge(fin_done, (i + 1) * (NB // G) // STORES)
                rows = slice(i * NB // STORES, (i + 1) * NB // STORES)
                sp.dma_start(out_view[:, rows, :], fin[:, rows, :]).then_inc(out_stored, 16)
            sp.wait_ge(out_stored, 16 * STORES)

        @block.gpsimd
        def _(pool):
            def load(k, s):
                if s >= ADJ_SLOTS:
                    pool.wait_ge(gathered, k - (ADJ_SLOTS - 1))
                pool.dma_start(adj_ring[s % ADJ_SLOTS][:, :],
                               adj_blocks[:, bass.ds(k, 1), :].rearrange("p o m -> p (o m)"))\
                    .then_inc(adj_in[s % ADJ_SLOTS], 16)

            nc.gpsimd.memset(ident[:, :], 0.0).then_inc(consts, 1)
            pool.wait_ge(consts, 1)
            nc.gpsimd.affine_select(out=ident[:, :], in_=ident[:, :], compare_op=ALU.not_equal, fill=1.0,
                                    base=0, pattern=[[-1, P]], channel_multiplier=1).then_inc(consts, 1)
            for k in range(AHEAD):
                load(k, k)
            nc.gpsimd.memset(ve[:, :, D:E], 1.0).then_inc(consts, 1)
            nc.gpsimd.memset(h2hi[:, :, D:E], H2SCALE).then_inc(consts, 1)
            nc.gpsimd.memset(minus_half[:, :], -0.5).then_inc(consts, 1)
            pool.wait_ge(consts, 5)

            def wait(*pairs):
                wait_all(pool, (consts, 5), *pairs)

            def residual(q, s):
                wait((hp_done, q + 1), *[(exp_done, q)] * (s >= 1))
                nc.gpsimd.tensor_scalar(hp_low[:, :], hp[:, :], 0.0, None, ALU.min).then_inc(low_done, 1)
                wait(*[(x1_done, q)] * (s >= 1))
                nc.gpsimd.tensor_scalar(hp_pos[:, :], hp[:, :], 0.0, None, ALU.max).then_inc(pos_done, 1)
                wait((exp_done, q + 1), (pos_done, q + 1))
                nc.gpsimd.tensor_tensor(elu[:, :], hp_exp[:, :], hp_pos[:, :], ALU.add).then_inc(sum_done, 1)
                wait((sum_done, q + 1))
                nc.gpsimd.tensor_scalar(hp_pos[:, :], elu[:, :], -1.0, None, ALU.add).then_inc(elu_done, 1)
                wait((elu_done, q + 1), *[(x1_kept, q), (norm_done, q)] * (s >= 1))
                nc.gpsimd.tensor_tensor(x1_now[:, :], hp_pos[:, :], at(x_sb, q), ALU.add).then_inc(x1_done, 1)
                wait((x1_done, q + 1))
                nc.gpsimd.tensor_copy(at(x1, q), x1_now[:, :]).then_inc(x1_kept, 1)

            def normalise(q, s):
                wait((mv_done, q + 1))
                nc.gpsimd.tensor_scalar(var_eps[:, :], mv[:, 1:2], EPS, None, ALU.add).then_inc(eps_done, 1)
                wait((eps_done, q + 1))
                nc.gpsimd.tensor_tensor(rstd2[:, 0:1], var_eps[:, :], minus_half[:, :], ALU.pow).then_inc(pow_done, 1)
                wait((pow_done, q + 1))
                nc.gpsimd.tensor_scalar(rstd2[:, 1:2], rstd2[:, 0:1], H2SCALE, None, ALU.mult).then_inc(rstd_done, 1)
                wait((rstd_done, q + 1), *[(relu_done, q)] * (s >= 1))
                nc.gpsimd.tensor_scalar(h2c[:, :], x1_now[:, :], mv[:, 0:1], rstd2[:, 1:2],
                                        ALU.subtract, ALU.mult).then_inc(norm_done, 1)
                wait((norm_done, q + 1), *[(hi_done, q), (lo_done, q)] * (s >= 1))
                nc.gpsimd.tensor_scalar(h2s[:, :], h2c[:, :], 0.0, None, ALU.max).then_inc(relu_done, 1)
                wait((relu_done, q + 1), *[(gathered, q - 1)] * (s >= 2))
                nc.gpsimd.tensor_copy(h2hi[:, s % 2, 0:D], h2s[:, :]).then_inc(hi_done, 1)
                wait((hi_done, q + 1))
                nc.gpsimd.tensor_tensor(h2lo[:, s % 2, :], h2s[:, :], h2hi[:, s % 2, 0:D], ALU.subtract)\
                    .then_inc(lo_done, 1)

            def step(k, s, turn):
                if s + AHEAD < NB:
                    load(k + AHEAD, s + AHEAD)
                if live(s, LAG):
                    residual(k - LAG, s - LAG)
                    normalise(k - LAG, s - LAG)

            run_steps(pool, step)

        @block.scalar
        def _(act):
            act.wait_ge(small_in, 48)
            for h in range(2):
                nc.scalar.activation(a_rep[:, h, :], a_sb[:, h:h + 1].to_broadcast([D, P]), ACT.Copy)\
                    .then_inc(a_repeated, 1)
            act.wait_ge(wu_turned, 1)
            nc.scalar.activation(wt[:, :], tb[0][0:D, 0:D], ACT.Copy).then_inc(wu_copied, 1)
            nc.scalar.activation(ut[:, :], tb[0][0:D, D:2 * D], ACT.Copy).then_inc(wu_copied, 1)
            act.wait_ge(wa_made, 1)
            nc.scalar.activation(wa1_row[:, :], tb[1][:, 0:D], ACT.Copy).then_inc(wa_copied, 1)
            nc.scalar.activation(wa2_rep[:, :], tb[1][0:D, P:2 * P], ACT.Copy).then_inc(wa_copied, 1)
            for g in range(NG):
                act.wait_ge(v_turned, g + 1)
                if g >= 2:
                    act.wait_ge(t_made, g - 1)
                nc.scalar.activation(vt[:, g % 2, :], tb[g % 2][0:D, :], ACT.Copy).then_inc(v_copied, 1)
                if g >= 1:
                    act.wait_ge(t_made, g)
                    nc.scalar.activation(t_row[:, (g - 1) * 512:g * 512], sums[(g - 1) % 2][:, :], ACT.Copy)\
                        .then_inc(t_copied, 1)
            act.wait_ge(t_made, NG)
            nc.scalar.activation(t_row[:, (NG - 1) * 512:], sums[(NG - 1) % 2][:, :], ACT.Copy).then_inc(t_copied, 1)
            act.wait_ge(ln1, LN1_VAR)
            nc.scalar.activation(root1[:, :], var1[:, :], ACT.Sqrt).then_inc(root_done, 1)

            def relu(q, s, half):
                part = slice(half * HALF, (half + 1) * HALF)
                wait_all(act, (s_done, 1), (w_done, q + 1),
                         *[(transposed, (q - (R_SLOTS - 1)) * NG)] * (s >= R_SLOTS and half == 0))
                nc.scalar.activation(r[s % R_SLOTS][:, part], w[s % W_SLOTS][:, part], ACT.Relu,
                                     bias=s_high[:, bass.ds(q, 1)], scale=1.0 - SLOPE).then_inc(relu_z, 1)

            def exponentials(q, s, g):
                act.wait_ge(transposed, q * NG + (g + 1))
                if s * NG + g >= PT_SLOTS:
                    act.wait_ge(attended, q * NG + (g + 1 - PT_SLOTS))
                nc.scalar.activation(pt[:, g % PT_SLOTS, :], tb[g % T_BANKS][:, :], ACT.Exp).then_inc(weights, 1)

            def elu_exp(q, s):
                act.wait_ge(low_done, q + 1)
                if s >= 1:
                    act.wait_ge(sum_done, q)
                nc.scalar.activation(hp_exp[:, :], hp_low[:, :], ACT.Exp).then_inc(exp_done, 1)

            def step(k, s, turn):
                for g in range(NG):
                    if live(s, 1) and g in RELU_AT:
                        relu(k - 1, s - 1, RELU_AT.index(g))
                    if live(s, LAG) and g == ELU_AT:
                        elu_exp(k - LAG, s - LAG)
                    if live(s, 2):
                        exponentials(k - 2, s - 2, g)

            run_steps(act, step)

            for g in range(NB // G):
                act.wait_ge(agg_turned, g + 1)
                if g >= 2:
                    act.wait_ge(product_done, g - 1)
                nc.scalar.activation(aggt[:, g % 2, :], tb[g % 2][0:D, :], ACT.Copy).then_inc(aggt_copied, 1)

        @block.vector
        def _(dve):
            n = [0]

            def chain(instruction):
                n[0] += 1
                instruction.then_inc(ln1, 1)
                dve.wait_ge(ln1, n[0])

            def wide(col):
                return col[:, :].unsqueeze(2).to_broadcast([P, NB, D])

            dve.wait_ge(x_in, 16)
            chain(nc.vector.tensor_reduce(mean1[:, :], x_sb[:, :, :], AX.X, ALU.add))
            chain(nc.vector.tensor_scalar(mean1[:, :], mean1[:, :], 1.0 / D, None, ALU.mult))
            chain(nc.vector.tensor_tensor(h1[:, :, :], x_sb[:, :, :], wide(mean1), ALU.subtract))
            chain(nc.vector.tensor_tensor(work[:, :, :], h1[:, :, :], h1[:, :, :], ALU.mult))
            chain(nc.vector.tensor_reduce(tmp1[:, :], work[:, :, :], AX.X, ALU.add))
            chain(nc.vector.tensor_scalar(var1[:, :], tmp1[:, :], 1.0 / D, EPS, ALU.mult, ALU.add))
            assert n[0] == LN1_VAR
            dve.wait_ge(root_done, 1)
            chain(nc.vector.reciprocal(rstd1[:, :], root1[:, :]))
            chain(nc.vector.tensor_tensor(tmp1[:, :], rstd1[:, :], rstd1[:, :], ALU.mult))
            chain(nc.vector.tensor_tensor(tmp1[:, :], tmp1[:, :], var1[:, :], ALU.mult))
            chain(nc.vector.tensor_scalar(tmp1[:, :], tmp1[:, :], -0.5, 1.5, ALU.mult, ALU.add))
            chain(nc.vector.tensor_tensor(rstd1[:, :], tmp1[:, :], rstd1[:, :], ALU.mult))
            chain(nc.vector.tensor_tensor(h1[:, :, :], h1[:, :, :], wide(rstd1), ALU.mult))
            chain(nc.vector.tensor_scalar(h1[:, :, :], h1[:, :, :], 0.0, None, ALU.max))
            dve.wait_ge(wa_copied, 2)
            chain(nc.vector.tensor_tensor(work[:, :, :], h1[:, :, :],
                                          wa1_row[:, :].unsqueeze(1).to_broadcast([P, NB, D]), ALU.mult))
            chain(nc.vector.tensor_reduce(s_col[:, :], work[:, :, :], AX.X, ALU.add))
            nc.vector.tensor_scalar(s_low[:, :], s_col[:, :], SLOPE, None, ALU.mult)
            nc.vector.tensor_scalar(s_high[:, :], s_col[:, :], 1.0 - SLOPE, None, ALU.mult).then_inc(s_done, 1)

            def make_mask(k, s, turn):
                dve.wait_ge(adj_in[s % ADJ_SLOTS], turn * 16 + 16 * (s // ADJ_SLOTS + 1))
                if s >= 1:
                    dve.wait_ge(w_done, k)
                nc.vector.tensor_scalar(mask[:, :], adj_ring[s % ADJ_SLOTS][:, :], 0.0, MASKED, ALU.is_le, ALU.mult)\
                    .then_inc(mask_done, 1)

            def add_mask(k, s):
                wait_all(dve, (t_copied, NG), (mask_done, k + 1),
                         *[(transposed, (k - (W_SLOTS - 1)) * NG)] * (s >= W_SLOTS), *[(z_done, k)] * (s >= 1))
                nc.vector.tensor_tensor_reduce(
                    out=w[s % W_SLOTS][:, :], in0=mask[:, :], in1=t_row[:, :], scale=1.0,
                    scalar=-3.0e38, op0=ALU.add, op1=ALU.max, accum_out=w_max[:, :]).then_inc(w_done, 1)

            def offsets(k, s):
                dve.wait_ge(s_done, 1)
                dve.wait_ge(w_done, k + 1)
                nc.vector.tensor_scalar(z_max[:, :], w_max[:, :], s_col[:, bass.ds(k, 1)], None, ALU.add).then_inc(z_done, 1)
                dve.wait_ge(z_done, k + 1)
                nc.vector.scalar_tensor_tensor(out=m_col[:, :], in0=z_max[:, :], scalar=SLOPE, in1=z_max[:, :],
                                               op0=ALU.mult, op1=ALU.max).then_inc(m_done, 1)
                dve.wait_ge(m_done, k + 1)
                nc.vector.tensor_scalar(c_col[:, s % 2:s % 2 + 1], m_col[:, :], -1.0, s_low[:, bass.ds(k, 1)],
                                        ALU.mult, ALU.add).then_inc(c_done, 1)

            def lower(q, s):
                dve.wait_ge(relu_z, 2 * q + 2)
                dve.wait_ge(c_done, q + 1)
                nc.vector.tensor_scalar(w[s % W_SLOTS][:, :], w[s % W_SLOTS][:, :], SLOPE, c_col[:, s % 2:s % 2 + 1],
                                        ALU.mult, ALU.add).then_inc(lowered, 1)

            def divide(q, s):
                dve.wait_ge(attended, q * NG + NG)
                nc.vector.reciprocal(rden[:, :], att[:, D:E]).then_inc(rden_done, 1)
                dve.wait_ge(rden_done, q + 1)
                if s >= 1:
                    dve.wait_ge(pos_done, q)
                nc.vector.scalar_tensor_tensor(out=hp[:, :], in0=att[:, 0:D], scalar=rden[:, 0:1], in1=at(h1, q),
                                               op0=ALU.mult, op1=ALU.add).then_inc(hp_done, 1)

            def statistics(q, s):
                dve.wait_ge(x1_done, q + 1)
                nc.vector.bn_stats(stats[:, :], x1_now[:, :]).then_inc(stats_done, 1)
                dve.wait_ge(x_in, 16)
                dve.wait_ge(stats_done, q + 1)
                if s >= 1:
                    dve.wait_ge(norm_done, q)
                nc.vector.bn_aggr(mv[:, :], stats[:, :]).then_inc(mv_done, 1)

            def step(k, s, turn):
                if live(s, LAG):
                    divide(k - LAG, s - LAG)
                if live(s, 0):
                    make_mask(k, s, turn)
                    add_mask(k, s)
                    offsets(k, s)
                if live(s, LAG):
                    statistics(k - LAG, s - LAG)
                if live(s, 1):
                    lower(k - 1, s - 1)

            run_steps(dve, step)

            dve.wait_ge(gathered, NB)
            for b in range(NSUM):
                c0, m = b * CB, min(CB, NB - b * CB)
                bank = sums[b][:, 0:m * E].rearrange("p (c e) -> p c e", e=E)
                nc.vector.reciprocal(rdeg[:, c0:c0 + m], bank[:, :, D:E].rearrange("p c o -> p (c o)"))\
                    .then_inc(rdeg_done, 1)
                dve.wait_ge(rdeg_done, b + 1)
                nc.vector.tensor_tensor(agg[:, c0:c0 + m, :], bank[:, :, 0:D],
                                        rdeg[:, c0:c0 + m].unsqueeze(2).to_broadcast([P, m, D]), ALU.mult)\
                    .then_inc(agg_done, 1)
            dve.wait_ge(x1_kept, NB)
            for g in range(NB // G):
                dve.wait_ge(product_done, g + 1)
                nc.vector.scalar_tensor_tensor(out=fin[:, g * G:(g + 1) * G, :],
                                               in0=sums[g % 2][:, 0:G * D].rearrange("p (c d) -> p c d", d=D),
                                               scalar=0.0, in1=x1[:, g * G:(g + 1) * G, :],
                                               op0=ALU.max, op1=ALU.add).then_inc(fin_done, 1)

        @block.tensor
        def _(pe):
            def turn_over(out_ap, in_ap, rows=P):
                return nc.tensor.transpose(out_ap, in_ap, ident[0:rows, 0:rows])

            pe.wait_ge(consts, 2)
            pe.wait_ge(small_in, 48)
            turn_over(tb[0][0:D, 0:D], w_sb[:, :], D)
            turn_over(tb[0][0:D, D:2 * D], u_sb[:, :], D).then_inc(wu_turned, 1)
            pe.wait_ge(a_repeated, 2)
            pe.wait_ge(wu_copied, 2)
            nc.tensor.matmul(tb[1][:, 0:D], a_rep[:, 0, :], wt[:, :], start=True, stop=True)
            nc.tensor.matmul(tb[1][0:D, P:2 * P], wt[:, :], a_rep[:, 1, :], start=True, stop=True).then_inc(wa_made, 1)
            pe.wait_ge(v_in, 16)
            pe.wait_ge(wa_copied, 2)

            def make_t(g):
                pe.wait_ge(v_copied, g + 1)
                if g >= 2:
                    pe.wait_ge(t_copied, g - 1)
                nc.tensor.matmul(sums[g % 2][:, :], wa2_rep[:, :], vt[:, g % 2, :], start=True, stop=True)\
                    .then_inc(t_made, 1)

            for g in range(NG):
                if g >= 2:
                    pe.wait_ge(v_copied, g - 1)
                for i in range(G):
                    last = turn_over(tb[g % 2][0:D, i * P:(i + 1) * P], ve[:, g * G + i, 0:D])
                last.then_inc(v_turned, 1)
                if g >= 1:
                    make_t(g - 1)
            make_t(NG - 1)
            pe.wait_ge(consts, 5)
            pe.wait_ge(t_copied, NG)

            def transposes(q, s, g):
                pe.wait_ge(relu_z, 2 * q + (1 if g < NG // 2 else 2))
                pe.wait_ge(lowered, q + 1)
                if s == 0 and g < T_BANKS:
                    pe.wait_ge(v_copied, NG)
                else:
                    pe.wait_ge(weights, q * NG + (g + 1 - T_BANKS))
                for i in range(G):
                    part = slice((g * G + i) * P, (g * G + i + 1) * P)
                    place = tb[g % T_BANKS][:, i * P:(i + 1) * P]
                    nc.tensor.matmul(place, r[s % R_SLOTS][:, part], ident[:, :], is_transpose=True, start=True, stop=False)
                    last = nc.tensor.matmul(place, w[s % W_SLOTS][:, part], ident[:, :], is_transpose=True,
                                            start=False, stop=True)
                last.then_inc(transposed, 1)

            def attend(q, s, g):
                pe.wait_ge(weights, q * NG + (g + 1))
                if g == 0 and s >= 1:
                    pe.wait_ge(hp_done, q)
                for i in range(G):
                    c = g * G + i
                    last = nc.tensor.matmul(att[:, 0:E], pt[:, g % PT_SLOTS, i * P:(i + 1) * P], ve[:, c, :],
                                            start=(c == 0), stop=(c == NC - 1))
                last.then_inc(attended, 1)

            def gather(q, s, chunks):
                if chunks[0] == 0:
                    pe.wait_ge(lo_done, q + 1)
                    pe.wait_ge(hi_done, q + 1)
                for c in chunks:
                    columns = adj_ring[s % ADJ_SLOTS][:, c * P:(c + 1) * P]
                    bank, at0 = sums[c // CB], (c % CB) * E
                    nc.tensor.matmul(bank[:, at0:at0 + E], columns, h2hi[:, s % 2, :],
                                     start=(s == 0 and c % CB == 0), stop=False, skip_group_check=True)
                    last = nc.tensor.matmul(bank[:, at0:at0 + D], columns, h2lo[:, s % 2, :],
                                            start=False, stop=(s == NB - 1), skip_group_check=True)
                if chunks[-1] == NC - 1:
                    last.then_inc(gathered, 1)

            def step(k, s, turn):
                for g in range(NG):
                    if live(s, 2):
                        transposes(k - 2, s - 2, g)
                        if g >= 1:
                            attend(k - 2, s - 2, g - 1)
                    if live(s, LAG) and g >= NG // 2:
                        per = 2 * NC // NG
                        first = (g - NG // 2) * per
                        gather(k - LAG, s - LAG, range(first, first + per))
                if live(s, 2):
                    attend(k - 2, s - 2, NG - 1)

            run_steps(pe, step)

            def product(g):
                pe.wait_ge(aggt_copied, g + 1)
                if g >= 2:
                    pe.wait_ge(fin_done, g - 1)
                for i in range(G):
                    last = nc.tensor.matmul(sums[g % 2][:, i * D:(i + 1) * D], aggt[:, g % 2, i * P:(i + 1) * P],
                                            ut[:, :], start=True, stop=True)
                last.then_inc(product_done, 1)

            for g in range(NB // G):
                pe.wait_ge(agg_done, min(NSUM, ((g + 1) * G - 1) // CB + 1) if g else 2)
                if g >= 2:
                    pe.wait_ge(aggt_copied, g - 1)
                for i in range(G):
                    last = turn_over(tb[g % 2][0:D, i * P:(i + 1) * P], agg[:, g * G + i, :])
                last.then_inc(agg_turned, 1)
                if g >= 1:
                    product(g - 1)
            product(NB // G - 1)


_INS = ['x', 'adj', 'L0_gnn_entity_embs', 'L0_gnn_W', 'L0_gnn_a', 'L1_gnn_U']
_OUTS = [((4096, 64), 'float32')]


def kernel(**inputs):
    import numpy as _np
    import concourse.bacc as _bacc
    from concourse import mybir as _mybir
    from concourse.bass_utils import run_bass_kernel_spmd as _run

    nc = _bacc.Bacc("TRN2", target_bir_lowering=False, num_devices=1)
    arrays, args = {}, []
    for name in _INS:
        a = _np.ascontiguousarray(inputs[name])
        arrays[f"in_{name}_dram"] = a
        args.append(nc.dram_tensor(f"in_{name}_dram", a.shape, _mybir.dt.from_np(a.dtype), kind="ExternalInput").ap())
    for i, (shape, dtype) in enumerate(_OUTS):
        dt = _mybir.dt.from_np(_np.dtype(dtype))
        args.append(nc.dram_tensor(f"out_{i}_dram", shape, dt, kind="ExternalOutput").ap())
    graph_layers_kernel(nc, *args)
    r = _run(nc, [arrays], core_ids=[0])
    return r.results[0]["out_0_dram"]
```

```python
from contextlib import ExitStack

import concourse.bass as bass
from concourse import mybir



def graph_layers_kernel(nc: bass.Bass, x, adj, V, W, a, U, out):
    fp32, fp16, bf16 = mybir.dt.float32, mybir.dt.float16, mybir.dt.bfloat16
    ALU = mybir.AluOpType
    ACT = mybir.ActivationFunctionType
    AX = mybir.AxisListType

    P = 128
    N, D = x.shape
    M = V.shape[0]
    NB = N // P
    NC = M // P
    G = 4
    NG = NC // G
    E = D + 1
    CB = 512 // E
    NSUM = -(-NB // CB)
    CLOSE, GATHER = 3, 4
    UNROLL = 6
    LOOPS = (NB - GATHER) // UNROLL
    AHEAD = 2
    BODY = NB - AHEAD - LOOPS * UNROLL
    SLOPE = 0.2
    MASKED = -float(2 ** 53)
    EPS = 1e-5
    H2SCALE = 4096.0
    QUARTER = M // 4
    ADJ_SLOTS, W_SLOTS, PT_SLOTS, T_BANKS = 6, 3, 4, 2
    EXP_AT, ELU_AT = (0, 2, 4, 6), 3
    STORES = 4
    LN1_VAR = 6

    adj_blocks = adj.rearrange("(k p) m -> p k m", p=P)
    x_view = x.rearrange("(k p) d -> p k d", p=P)
    v_view = V.rearrange("(c p) d -> p c d", p=P)
    out_view = out.rearrange("(k p) d -> p k d", p=P)

    ctx = ExitStack()
    with ctx:
        def sb(name, shape, dt=fp32):
            return ctx.enter_context(nc.sbuf_tensor(name, shape, dt))

        def sem(name):
            return ctx.enter_context(nc.semaphore(name))

        adj_ring = [sb(f"adj{i}", [P, M], bf16) for i in range(ADJ_SLOTS)]
        w = [sb(f"w{i}", [P, M]) for i in range(W_SLOTS)]
        mask = sb("mask", [P, M], bf16)
        t_row = sb("t_row", [P, M])
        t_low = sb("t_low", [P, M])
        pt = sb("pt", [P, PT_SLOTS, G * P])
        ident = sb("ident", [P, P])
        x_sb = sb("x_sb", [P, NB, D])
        h1 = sb("h1", [P, NB, D])
        x1 = sb("x1", [P, NB, D])
        ve = sb("ve", [P, NC, E])
        vt = sb("vt", [D, 2, G * P])
        work = w[2][:, 0:NB * D].rearrange("p (k d) -> p k d", d=D)
        w_sb = sb("w_sb", [D, D])
        u_sb = sb("u_sb", [D, D])
        a_sb = sb("a_sb", [D, 2])
        a_rep = sb("a_rep", [D, 2, P])
        wt = sb("wt", [D, D])
        ut = sb("ut", [D, D])
        wa1_row = sb("wa1_row", [P, D])
        wa2_rep = sb("wa2_rep", [D, P])
        s_col = sb("s_col", [P, NB])
        s_high = sb("s_high", [P, NB])
        mean1 = sb("mean1", [P, NB])
        var1 = sb("var1", [P, NB])
        root1 = sb("root1", [P, NB])
        rstd1 = sb("rstd1", [P, NB])
        tmp1 = sb("tmp1", [P, NB])
        w_max = sb("w_max", [P, 1])
        neg_max = sb("neg_max", [P, 2])
        rden = sb("rden", [P, 1])
        hp = sb("hp", [P, D])
        x1_now = sb("x1_now", [P, D])
        hp_low = sb("hp_low", [P, D])
        hp_exp = sb("hp_exp", [P, D])
        hp_pos = sb("hp_pos", [P, D])
        elu = sb("elu", [P, D])
        stats = sb("stats", [P, 6])
        mv = sb("mv", [P, 2])
        var_eps = sb("var_eps", [P, 1])
        rstd2 = sb("rstd2", [P, 2])
        minus_half = sb("minus_half", [P, 1])
        h2s = sb("h2s", [P, D])
        h2c = sb("h2c", [P, D])
        h2hi = sb("h2hi", [P, 2, E], fp16)
        h2lo = sb("h2lo", [P, 2, D], fp16)
        rdeg = sb("rdeg", [P, NB])
        agg = work
        aggt = sb("aggt", [D, 2, G * P])
        fin = h1

        sums = [ctx.enter_context(nc.psum_tensor(f"sums{i}", [P, 512], fp32)) for i in range(NSUM)]
        tb = [ctx.enter_context(nc.psum_tensor(f"tb{i}", [P, 512], fp32)) for i in range(T_BANKS)]
        att = ctx.enter_context(nc.psum_tensor("att", [P, 512], fp32))

        adj_in = [sem(f"adj_in{i}") for i in range(ADJ_SLOTS)]
        small_in, v_in, x_in, out_stored = sem("small_in"), sem("v_in"), sem("x_in"), sem("out_stored")
        consts = sem("consts")
        a_repeated = sem("a_repeated")
        wu_turned = sem("wu_turned")
        wu_copied = sem("wu_copied")
        wa_made = sem("wa_made")
        wa_copied = sem("wa_copied")
        v_turned = sem("v_turned")
        v_copied = sem("v_copied")
        t_made = sem("t_made")
        t_copied = sem("t_copied")
        t_low_done = sem("t_low_done")
        ln1 = sem("ln1")
        root_done = sem("root_done")
        s_done = sem("s_done")
        mask_done = sem("mask_done")
        leaky_done = sem("leaky_done")
        w_done = sem("w_done")
        max_neg = sem("max_neg")
        exp_w = sem("exp_w")
        transposed = sem("transposed")
        weights = sem("weights")
        attended = sem("attended")
        rden_done = sem("rden_done")
        hp_done = sem("hp_done")
        low_done = sem("low_done")
        pos_done = sem("pos_done")
        exp_done = sem("exp_done")
        sum_done = sem("sum_done")
        elu_done = sem("elu_done")
        x1_done = sem("x1_done")
        x1_kept = sem("x1_kept")
        stats_done = sem("stats_done")
        mv_done = sem("mv_done")
        eps_done = sem("eps_done")
        pow_done = sem("pow_done")
        rstd_done = sem("rstd_done")
        norm_done = sem("norm_done")
        relu_done = sem("relu_done")
        hi_done = sem("hi_done")
        lo_done = sem("lo_done")
        gathered = sem("gathered")
        rdeg_done = sem("rdeg_done")
        agg_done = sem("agg_done")
        agg_turned = sem("agg_turned")
        aggt_copied = sem("aggt_copied")
        product_done = sem("product_done")
        fin_done = sem("fin_done")

        block = ctx.enter_context(nc.Block())

        def run_steps(engine, step):
            for k in range(BODY):
                step(k, k, 0)
            with engine.Fori(0, LOOPS) as it:
                for u in range(UNROLL):
                    step(it * UNROLL + (BODY + u), BODY + u, it)
            for k in range(BODY + LOOPS * UNROLL, NB + GATHER):
                step(k, k, 0)

        def wait_all(engine, ready, *pairs):
            for _, value in pairs:
                if not isinstance(value, int):
                    engine.compute_val(value)
            engine.wait_ge(*ready)
            for semaphore, value in pairs:
                engine.wait_ge(semaphore, value)

        def live(s, lag):
            return lag <= s < NB + lag

        def at(tensor, q):
            return tensor[:, bass.ds(q, 1), :].rearrange("p o d -> p (o d)")

        @block.sync
        def _(sp):
            sp.dma_start(w_sb[:, :], W[:, :]).then_inc(small_in, 16)
            sp.dma_start(u_sb[:, :], U[:, :]).then_inc(small_in, 16)
            with nc.allow_non_contiguous_dma(reason="2 x 64 numbers"):
                sp.dma_start(a_sb[:, :], a.rearrange("(h d) o -> d (h o)", h=2)).then_inc(small_in, 16)
            sp.dma_start(ve[:, :, 0:D], v_view).then_inc(v_in, 16)
            sp.dma_start(x_sb[:, :, :], x_view).then_inc(x_in, 16)
            for i in range(STORES):
                sp.wait_ge(fin_done, (i + 1) * (NB // G) // STORES)
                rows = slice(i * NB // STORES, (i + 1) * NB // STORES)
                sp.dma_start(out_view[:, rows, :], fin[:, rows, :]).then_inc(out_stored, 16)
            sp.wait_ge(out_stored, 16 * STORES)

        @block.gpsimd
        def _(pool):
            def load(k, s):
                if s >= ADJ_SLOTS:
                    pool.wait_ge(gathered, k - (ADJ_SLOTS - 1))
                pool.dma_start(adj_ring[s % ADJ_SLOTS][:, :],
                               adj_blocks[:, bass.ds(k, 1), :].rearrange("p o m -> p (o m)"))\
                    .then_inc(adj_in[s % ADJ_SLOTS], 16)

            nc.gpsimd.memset(ident[:, :], 0.0).then_inc(consts, 1)
            pool.wait_ge(consts, 1)
            nc.gpsimd.affine_select(out=ident[:, :], in_=ident[:, :], compare_op=ALU.not_equal, fill=1.0,
                                    base=0, pattern=[[-1, P]], channel_multiplier=1).then_inc(consts, 1)
            for k in range(AHEAD):
                load(k, k)
            nc.gpsimd.memset(ve[:, :, D:E], 1.0).then_inc(consts, 1)
            nc.gpsimd.memset(h2hi[:, :, D:E], H2SCALE).then_inc(consts, 1)
            nc.gpsimd.memset(minus_half[:, :], -0.5).then_inc(consts, 1)
            pool.wait_ge(consts, 5)

            def wait(*pairs):
                wait_all(pool, (consts, 5), *pairs)

            def residual(q, s):
                wait((hp_done, q + 1), *[(exp_done, q)] * (s >= 1))
                nc.gpsimd.tensor_scalar(hp_low[:, :], hp[:, :], 0.0, None, ALU.min).then_inc(low_done, 1)
                wait(*[(x1_done, q)] * (s >= 1))
                nc.gpsimd.tensor_scalar(hp_pos[:, :], hp[:, :], 0.0, None, ALU.max).then_inc(pos_done, 1)
                wait((exp_done, q + 1), (pos_done, q + 1))
                nc.gpsimd.tensor_tensor(elu[:, :], hp_exp[:, :], hp_pos[:, :], ALU.add).then_inc(sum_done, 1)
                wait((sum_done, q + 1))
                nc.gpsimd.tensor_scalar(hp_pos[:, :], elu[:, :], -1.0, None, ALU.add).then_inc(elu_done, 1)
                wait((elu_done, q + 1), *[(x1_kept, q), (norm_done, q)] * (s >= 1))
                nc.gpsimd.tensor_tensor(x1_now[:, :], hp_pos[:, :], at(x_sb, q), ALU.add).then_inc(x1_done, 1)
                wait((x1_done, q + 1))
                nc.gpsimd.tensor_copy(at(x1, q), x1_now[:, :]).then_inc(x1_kept, 1)

            def normalise(q, s):
                wait((mv_done, q + 1))
                nc.gpsimd.tensor_scalar(var_eps[:, :], mv[:, 1:2], EPS, None, ALU.add).then_inc(eps_done, 1)
                wait((eps_done, q + 1))
                nc.gpsimd.tensor_tensor(rstd2[:, 0:1], var_eps[:, :], minus_half[:, :], ALU.pow).then_inc(pow_done, 1)
                wait((pow_done, q + 1))
                nc.gpsimd.tensor_scalar(rstd2[:, 1:2], rstd2[:, 0:1], H2SCALE, None, ALU.mult).then_inc(rstd_done, 1)
                wait((rstd_done, q + 1), *[(relu_done, q)] * (s >= 1))
                nc.gpsimd.tensor_scalar(h2c[:, :], x1_now[:, :], mv[:, 0:1], rstd2[:, 1:2],
                                        ALU.subtract, ALU.mult).then_inc(norm_done, 1)
                wait((norm_done, q + 1), *[(hi_done, q), (lo_done, q)] * (s >= 1))
                nc.gpsimd.tensor_scalar(h2s[:, :], h2c[:, :], 0.0, None, ALU.max).then_inc(relu_done, 1)
                wait((relu_done, q + 1), *[(gathered, q - 1)] * (s >= 2))
                nc.gpsimd.tensor_copy(h2hi[:, s % 2, 0:D], h2s[:, :]).then_inc(hi_done, 1)
                wait((hi_done, q + 1))
                nc.gpsimd.tensor_tensor(h2lo[:, s % 2, :], h2s[:, :], h2hi[:, s % 2, 0:D], ALU.subtract)\
                    .then_inc(lo_done, 1)

            def step(k, s, turn):
                if live(s, CLOSE):
                    residual(k - CLOSE, s - CLOSE)
                    normalise(k - CLOSE, s - CLOSE)
                if s + AHEAD < NB:
                    load(k + AHEAD, s + AHEAD)

            run_steps(pool, step)

        @block.scalar
        def _(act):
            act.wait_ge(small_in, 48)
            for h in range(2):
                nc.scalar.activation(a_rep[:, h, :], a_sb[:, h:h + 1].to_broadcast([D, P]), ACT.Copy)\
                    .then_inc(a_repeated, 1)
            act.wait_ge(wu_turned, 1)
            nc.scalar.activation(wt[:, :], tb[0][0:D, 0:D], ACT.Copy).then_inc(wu_copied, 1)
            nc.scalar.activation(ut[:, :], tb[0][0:D, D:2 * D], ACT.Copy).then_inc(wu_copied, 1)
            act.wait_ge(wa_made, 1)
            nc.scalar.activation(wa1_row[:, :], tb[1][:, 0:D], ACT.Copy).then_inc(wa_copied, 1)
            nc.scalar.activation(wa2_rep[:, :], tb[1][0:D, P:2 * P], ACT.Copy).then_inc(wa_copied, 1)
            for g in range(NG):
                act.wait_ge(v_turned, g + 1)
                if g >= 2:
                    act.wait_ge(t_made, g - 1)
                nc.scalar.activation(vt[:, g % 2, :], tb[g % 2][0:D, :], ACT.Copy).then_inc(v_copied, 1)
                if g >= 1:
                    act.wait_ge(t_made, g)
                    nc.scalar.activation(t_row[:, (g - 1) * 512:g * 512], sums[(g - 1) % 2][:, :], ACT.Copy)\
                        .then_inc(t_copied, 1)
            act.wait_ge(t_made, NG)
            nc.scalar.activation(t_row[:, (NG - 1) * 512:], sums[(NG - 1) % 2][:, :], ACT.Copy).then_inc(t_copied, 1)
            act.wait_ge(ln1, LN1_VAR)
            nc.scalar.activation(root1[:, :], var1[:, :], ACT.Sqrt).then_inc(root_done, 1)

            def exponentials(q, s, part):
                quarter = w[s % W_SLOTS][:, part * QUARTER:(part + 1) * QUARTER]
                act.wait_ge(w_done, q + 1)
                act.wait_ge(max_neg, q + 1)
                nc.scalar.activation(quarter, quarter, ACT.Exp, bias=neg_max[:, s % 2:s % 2 + 1]).then_inc(exp_w, 1)

            def evacuate(q, s, g):
                act.wait_ge(transposed, q * NG + (g + 1))
                if s * NG + g >= PT_SLOTS:
                    act.wait_ge(attended, q * NG + (g + 1 - PT_SLOTS))
                nc.scalar.activation(pt[:, g % PT_SLOTS, :], tb[g % T_BANKS][:, :], ACT.Copy).then_inc(weights, 1)

            def elu_exp(q, s):
                act.wait_ge(low_done, q + 1)
                if s >= 1:
                    act.wait_ge(sum_done, q)
                nc.scalar.activation(hp_exp[:, :], hp_low[:, :], ACT.Exp).then_inc(exp_done, 1)

            def step(k, s, turn):
                for g in range(NG):
                    if live(s, 1) and g in EXP_AT:
                        exponentials(k - 1, s - 1, EXP_AT.index(g))
                    if live(s, CLOSE) and g == ELU_AT:
                        elu_exp(k - CLOSE, s - CLOSE)
                    if live(s, 2):
                        evacuate(k - 2, s - 2, g)

            run_steps(act, step)

            for g in range(NB // G):
                act.wait_ge(agg_turned, g + 1)
                if g >= 2:
                    act.wait_ge(product_done, g - 1)
                nc.scalar.activation(aggt[:, g % 2, :], tb[g % 2][0:D, :], ACT.Copy).then_inc(aggt_copied, 1)

        @block.vector
        def _(dve):
            n = [0]

            def chain(instruction):
                n[0] += 1
                instruction.then_inc(ln1, 1)
                dve.wait_ge(ln1, n[0])

            def wide(col):
                return col[:, :].unsqueeze(2).to_broadcast([P, NB, D])

            dve.wait_ge(x_in, 16)
            chain(nc.vector.tensor_reduce(mean1[:, :], x_sb[:, :, :], AX.X, ALU.add))
            chain(nc.vector.tensor_scalar(mean1[:, :], mean1[:, :], 1.0 / D, None, ALU.mult))
            chain(nc.vector.tensor_tensor(h1[:, :, :], x_sb[:, :, :], wide(mean1), ALU.subtract))
            chain(nc.vector.tensor_tensor(work[:, :, :], h1[:, :, :], h1[:, :, :], ALU.mult))
            chain(nc.vector.tensor_reduce(tmp1[:, :], work[:, :, :], AX.X, ALU.add))
            chain(nc.vector.tensor_scalar(var1[:, :], tmp1[:, :], 1.0 / D, EPS, ALU.mult, ALU.add))
            assert n[0] == LN1_VAR
            dve.wait_ge(root_done, 1)
            chain(nc.vector.reciprocal(rstd1[:, :], root1[:, :]))
            chain(nc.vector.tensor_tensor(tmp1[:, :], rstd1[:, :], rstd1[:, :], ALU.mult))
            chain(nc.vector.tensor_tensor(tmp1[:, :], tmp1[:, :], var1[:, :], ALU.mult))
            chain(nc.vector.tensor_scalar(tmp1[:, :], tmp1[:, :], -0.5, 1.5, ALU.mult, ALU.add))
            chain(nc.vector.tensor_tensor(rstd1[:, :], tmp1[:, :], rstd1[:, :], ALU.mult))
            chain(nc.vector.tensor_tensor(h1[:, :, :], h1[:, :, :], wide(rstd1), ALU.mult))
            chain(nc.vector.tensor_scalar(h1[:, :, :], h1[:, :, :], 0.0, None, ALU.max))
            dve.wait_ge(wa_copied, 2)
            chain(nc.vector.tensor_tensor(work[:, :, :], h1[:, :, :],
                                          wa1_row[:, :].unsqueeze(1).to_broadcast([P, NB, D]), ALU.mult))
            chain(nc.vector.tensor_reduce(s_col[:, :], work[:, :, :], AX.X, ALU.add))
            nc.vector.tensor_scalar(s_high[:, :], s_col[:, :], 1.0 - SLOPE, None, ALU.mult).then_inc(s_done, 1)

            for g in range(NG):
                dve.wait_ge(t_copied, g + 1)
                part = slice(g * 512, (g + 1) * 512)
                nc.vector.tensor_scalar(t_low[:, part], t_row[:, part], SLOPE, None, ALU.mult).then_inc(t_low_done, 1)

            def make_mask(k, s, turn):
                dve.wait_ge(adj_in[s % ADJ_SLOTS], turn * 16 + 16 * (s // ADJ_SLOTS + 1))
                if s >= 1:
                    dve.wait_ge(w_done, k)
                nc.vector.tensor_scalar(mask[:, :], adj_ring[s % ADJ_SLOTS][:, :], 0.0, MASKED, ALU.is_le, ALU.mult)\
                    .then_inc(mask_done, 1)

            def leaky(k, s):
                dve.wait_ge(t_low_done, NG)
                if s >= W_SLOTS:
                    dve.wait_ge(transposed, (k - (W_SLOTS - 1)) * NG)
                nc.vector.scalar_tensor_tensor(out=w[s % W_SLOTS][:, :], in0=t_row[:, :],
                                               scalar=s_high[:, bass.ds(k, 1)], in1=t_low[:, :],
                                               op0=ALU.add, op1=ALU.max).then_inc(leaky_done, 1)

            def add_mask(k, s):
                wait_all(dve, (t_copied, NG), (mask_done, k + 1), (leaky_done, k + 1), *[(max_neg, k)] * (s >= 1))
                nc.vector.tensor_tensor_reduce(
                    out=w[s % W_SLOTS][:, :], in0=mask[:, :], in1=w[s % W_SLOTS][:, :], scale=1.0,
                    scalar=-3.0e38, op0=ALU.add, op1=ALU.max, accum_out=w_max[:, :]).then_inc(w_done, 1)

            def negate(k, s):
                dve.wait_ge(w_done, k + 1)
                if s >= 2:
                    dve.wait_ge(exp_w, 4 * (k - 1))
                nc.vector.tensor_scalar(neg_max[:, s % 2:s % 2 + 1], w_max[:, :], -1.0, None, ALU.mult)\
                    .then_inc(max_neg, 1)

            def divide(q, s):
                dve.wait_ge(attended, q * NG + NG)
                nc.vector.reciprocal(rden[:, :], att[:, D:E]).then_inc(rden_done, 1)
                dve.wait_ge(rden_done, q + 1)
                if s >= 1:
                    dve.wait_ge(pos_done, q)
                nc.vector.scalar_tensor_tensor(out=hp[:, :], in0=att[:, 0:D], scalar=rden[:, 0:1], in1=at(h1, q),
                                               op0=ALU.mult, op1=ALU.add).then_inc(hp_done, 1)

            def statistics(q, s):
                dve.wait_ge(x1_done, q + 1)
                nc.vector.bn_stats(stats[:, :], x1_now[:, :]).then_inc(stats_done, 1)
                dve.wait_ge(x_in, 16)
                dve.wait_ge(stats_done, q + 1)
                if s >= 1:
                    dve.wait_ge(norm_done, q)
                nc.vector.bn_aggr(mv[:, :], stats[:, :]).then_inc(mv_done, 1)

            def step(k, s, turn):
                if live(s, CLOSE):
                    divide(k - CLOSE, s - CLOSE)
                if live(s, 0):
                    make_mask(k, s, turn)
                    leaky(k, s)
                if live(s, CLOSE):
                    statistics(k - CLOSE, s - CLOSE)
                if live(s, 0):
                    add_mask(k, s)
                    negate(k, s)

            run_steps(dve, step)

            dve.wait_ge(gathered, NB)
            for b in range(NSUM):
                c0, m = b * CB, min(CB, NB - b * CB)
                bank = sums[b][:, 0:m * E].rearrange("p (c e) -> p c e", e=E)
                nc.vector.reciprocal(rdeg[:, c0:c0 + m], bank[:, :, D:E].rearrange("p c o -> p (c o)"))\
                    .then_inc(rdeg_done, 1)
                dve.wait_ge(rdeg_done, b + 1)
                nc.vector.tensor_tensor(agg[:, c0:c0 + m, :], bank[:, :, 0:D],
                                        rdeg[:, c0:c0 + m].unsqueeze(2).to_broadcast([P, m, D]), ALU.mult)\
                    .then_inc(agg_done, 1)
            dve.wait_ge(x1_kept, NB)
            for g in range(NB // G):
                dve.wait_ge(product_done, g + 1)
                nc.vector.scalar_tensor_tensor(out=fin[:, g * G:(g + 1) * G, :],
                                               in0=sums[g % 2][:, 0:G * D].rearrange("p (c d) -> p c d", d=D),
                                               scalar=0.0, in1=x1[:, g * G:(g + 1) * G, :],
                                               op0=ALU.max, op1=ALU.add).then_inc(fin_done, 1)

        @block.tensor
        def _(pe):
            def turn_over(out_ap, in_ap, rows=P):
                return nc.tensor.transpose(out_ap, in_ap, ident[0:rows, 0:rows])

            pe.wait_ge(consts, 2)
            pe.wait_ge(small_in, 48)
            turn_over(tb[0][0:D, 0:D], w_sb[:, :], D)
            turn_over(tb[0][0:D, D:2 * D], u_sb[:, :], D).then_inc(wu_turned, 1)
            pe.wait_ge(a_repeated, 2)
            pe.wait_ge(wu_copied, 2)
            nc.tensor.matmul(tb[1][:, 0:D], a_rep[:, 0, :], wt[:, :], start=True, stop=True)
            nc.tensor.matmul(tb[1][0:D, P:2 * P], wt[:, :], a_rep[:, 1, :], start=True, stop=True).then_inc(wa_made, 1)
            pe.wait_ge(v_in, 16)
            pe.wait_ge(wa_copied, 2)

            def make_t(g):
                pe.wait_ge(v_copied, g + 1)
                if g >= 2:
                    pe.wait_ge(t_copied, g - 1)
                nc.tensor.matmul(sums[g % 2][:, :], wa2_rep[:, :], vt[:, g % 2, :], start=True, stop=True)\
                    .then_inc(t_made, 1)

            for g in range(NG):
                if g >= 2:
                    pe.wait_ge(v_copied, g - 1)
                for i in range(G):
                    last = turn_over(tb[g % 2][0:D, i * P:(i + 1) * P], ve[:, g * G + i, 0:D])
                last.then_inc(v_turned, 1)
                if g >= 1:
                    make_t(g - 1)
            make_t(NG - 1)
            pe.wait_ge(consts, 5)
            pe.wait_ge(t_copied, NG)

            def transposes(q, s, g):
                pe.wait_ge(exp_w, 4 * q + (g // 2 + 1))
                if s == 0 and g < T_BANKS:
                    pe.wait_ge(v_copied, NG)
                else:
                    pe.wait_ge(weights, q * NG + (g + 1 - T_BANKS))
                for i in range(G):
                    c = g * G + i
                    last = turn_over(tb[g % T_BANKS][:, i * P:(i + 1) * P], w[s % W_SLOTS][:, c * P:(c + 1) * P])
                last.then_inc(transposed, 1)

            def attend(q, s, g):
                pe.wait_ge(weights, q * NG + (g + 1))
                if g == 0 and s >= 1:
                    pe.wait_ge(hp_done, q)
                for i in range(G):
                    c = g * G + i
                    last = nc.tensor.matmul(att[:, 0:E], pt[:, g % PT_SLOTS, i * P:(i + 1) * P], ve[:, c, :],
                                            start=(c == 0), stop=(c == NC - 1))
                last.then_inc(attended, 1)

            def gather(q, s, chunks):
                if chunks[0] == 0:
                    pe.wait_ge(lo_done, q + 1)
                    pe.wait_ge(hi_done, q + 1)
                for c in chunks:
                    columns = adj_ring[s % ADJ_SLOTS][:, c * P:(c + 1) * P]
                    bank, at0 = sums[c // CB], (c % CB) * E
                    nc.tensor.matmul(bank[:, at0:at0 + E], columns, h2hi[:, s % 2, :],
                                     start=(s == 0 and c % CB == 0), stop=False, skip_group_check=True)
                    last = nc.tensor.matmul(bank[:, at0:at0 + D], columns, h2lo[:, s % 2, :],
                                            start=False, stop=(s == NB - 1), skip_group_check=True)
                if chunks[-1] == NC - 1:
                    last.then_inc(gathered, 1)

            def step(k, s, turn):
                for g in range(NG):
                    if live(s, 2):
                        transposes(k - 2, s - 2, g)
                        if g >= 1:
                            attend(k - 2, s - 2, g - 1)
                    if live(s, GATHER):
                        gather(k - GATHER, s - GATHER, range(g * G, g * G + G))
                if live(s, 2):
                    attend(k - 2, s - 2, NG - 1)

            run_steps(pe, step)

            def product(g):
                pe.wait_ge(aggt_copied, g + 1)
                if g >= 2:
                    pe.wait_ge(fin_done, g - 1)
                for i in range(G):
                    last = nc.tensor.matmul(sums[g % 2][:, i * D:(i + 1) * D], aggt[:, g % 2, i * P:(i + 1) * P],
                                            ut[:, :], start=True, stop=True)
                last.then_inc(product_done, 1)

            for g in range(NB // G):
                pe.wait_ge(agg_done, min(NSUM, ((g + 1) * G - 1) // CB + 1) if g else 2)
                if g >= 2:
                    pe.wait_ge(aggt_copied, g - 1)
                for i in range(G):
                    last = turn_over(tb[g % 2][0:D, i * P:(i + 1) * P], agg[:, g * G + i, :])
                last.then_inc(agg_turned, 1)
                if g >= 1:
                    product(g - 1)
            product(NB // G - 1)


_INS = ['x', 'adj', 'L0_gnn_entity_embs', 'L0_gnn_W', 'L0_gnn_a', 'L1_gnn_U']
_OUTS = [((4096, 64), 'float32')]


def kernel(**inputs):
    import numpy as _np
    import concourse.bacc as _bacc
    from concourse import mybir as _mybir
    from concourse.bass_utils import run_bass_kernel_spmd as _run

    nc = _bacc.Bacc("TRN2", target_bir_lowering=False, num_devices=1)
    arrays, args = {}, []
    for name in _INS:
        a = _np.ascontiguousarray(inputs[name])
        arrays[f"in_{name}_dram"] = a
        args.append(nc.dram_tensor(f"in_{name}_dram", a.shape, _mybir.dt.from_np(a.dtype), kind="ExternalInput").ap())
    for i, (shape, dtype) in enumerate(_OUTS):
        dt = _mybir.dt.from_np(_np.dtype(dtype))
        args.append(nc.dram_tensor(f"out_{i}_dram", shape, dt, kind="ExternalOutput").ap())
    graph_layers_kernel(nc, *args)
    r = _run(nc, [arrays], core_ids=[0])
    return r.results[0]["out_0_dram"]
```

```python
from contextlib import ExitStack

import concourse.bass as bass
from concourse import mybir



def graph_layers_kernel(nc: bass.Bass, x, adj, V, W, a, U, out):
    fp32, fp16, bf16 = mybir.dt.float32, mybir.dt.float16, mybir.dt.bfloat16
    ALU = mybir.AluOpType
    ACT = mybir.ActivationFunctionType
    AX = mybir.AxisListType

    P = 128
    N, D = x.shape
    M = V.shape[0]
    NB = N // P
    NC = M // P
    G = 4
    NG = NC // G
    E = D + 1
    CB = 512 // E
    NSUM = -(-NB // CB)
    CLOSE, GATHER = 3, 4
    UNROLL = 6
    LOOPS = (NB - GATHER) // UNROLL
    AHEAD = 2
    BODY = NB - AHEAD - LOOPS * UNROLL
    SLOPE = 0.2
    MASKED = float(2 ** 53)
    EPS = 1e-5
    H2SCALE = 4096.0
    QUARTER = M // 4
    ADJ_SLOTS, W_SLOTS, PT_SLOTS, T_BANKS = 6, 3, 4, 2
    ATT_AT, RELU_AT, ELU_AT, EXP_AT = 2, 1, 3, (2, 3, 6, 7)
    HALVES = 2
    SPLIT = (0, 1)
    HG = NG // HALVES
    NS = len(SPLIT)
    WSCALE_LN = 7.624618986159398
    PARTS = 4
    PB = NB // PARTS

    LAG = 3
    GATHER_AT = ((), (), (), (0, 1), (2, 3), (4, 5), (6, 7), ())
    CONSTS = 7

    adj_blocks = adj.rearrange("(k p) m -> p k m", p=P)
    x_view = x.rearrange("(k p) d -> p k d", p=P)
    v_view = V.rearrange("(c p) d -> p c d", p=P)
    out_view = out.rearrange("(k p) d -> p k d", p=P)

    ctx = ExitStack()
    with ctx:
        def sb(name, shape, dt=fp32):
            return ctx.enter_context(nc.sbuf_tensor(name, shape, dt))

        def sem(name):
            return ctx.enter_context(nc.semaphore(name))

        adj_ring = [sb(f"adj{i}", [P, M], bf16) for i in range(ADJ_SLOTS)]
        w = [sb(f"w{i}", [P, M]) for i in range(W_SLOTS)]
        mask = sb("mask", [P, M], bf16)
        t_row = sb("t_row", [P, M])
        t_low = sb("t_low", [P, M])
        pt = sb("pt", [P, PT_SLOTS, G * P])
        pt_hi = sb("pt_hi", [P, NS, G * P], fp16)
        pt_lo = sb("pt_lo", [P, NS, G * P], fp16)
        ident = sb("ident", [P, P])
        x_sb = sb("x_sb", [P, NB, D])
        h1 = sb("h1", [P, NB, D])
        x1 = sb("x1", [P, NB, D])
        ve = sb("ve", [P, NC, E])
        v16 = sb("v16", [P, HALVES, NS * G, E + 2 * D], bf16)
        v_split = ve[:, :, 0:D].rearrange("p (h c) d -> p h c d", h=HALVES)[:, :, 0:NS * G, :]
        v_rest = w[2][:, 0:HALVES * NS * G * D].rearrange("p (h c d) -> p h c d", h=HALVES, d=D)
        v16_parts = [slice(0, D), slice(E, E + D), slice(E + D, E + 2 * D)]
        vt = w[1][0:D, :].rearrange("p (g c) -> p g c", g=NG)
        work = x1
        w_sb = sb("w_sb", [D, D])
        u_sb = sb("u_sb", [P, P])
        a_all = sb("a_all", [D, 2, D])
        w_times_a = sb("w_times_a", [D, 2, D])
        wa_sb = sb("wa_sb", [D, 2])
        wa_rep = sb("wa_rep", [D, 2, P])
        ut = sb("ut", [P, P])
        wa1_row = sb("wa1_row", [P, D])
        s_high = sb("s_high", [P, NB])
        mean1 = sb("mean1", [P, NB])
        var1 = sb("var1", [P, NB])
        rstd1 = sb("rstd1", [P, NB])
        tmp1 = sb("tmp1", [P, NB])
        w_min = sb("w_min", [P, 2])
        bias = sb("bias", [P, 2])
        wscale_ln = sb("wscale_ln", [P, 1])
        att_sb = sb("att_sb", [P, 2, E])
        rden = sb("rden", [P, 1])
        hp = sb("hp", [P, D])
        x1_now = sb("x1_now", [P, D])
        hp_low = sb("hp_low", [P, D])
        hp_exp = sb("hp_exp", [P, D])
        hp_pos = sb("hp_pos", [P, D])
        elu = sb("elu", [P, D])
        stats = sb("stats", [P, 6])
        mv = sb("mv", [P, 2])
        var_eps = sb("var_eps", [P, 1])
        rstd2 = sb("rstd2", [P, 1])
        minus_half = sb("minus_half", [P, PB])
        h2s = sb("h2s", [P, D])
        h2c = sb("h2c", [P, D])
        h2hi = sb("h2hi", [P, 2, E], fp16)
        h2lo = sb("h2lo", [P, 2, D], fp16)
        rdeg = sb("rdeg", [P, NB])
        agg = w[2][:, 0:NB * D].rearrange("p (k d) -> p k d", d=D)
        aggt = w[0][:, 0:NB // 2 * P].rearrange("p (g c) -> p g c", g=PARTS)
        fin = h1

        sums = [ctx.enter_context(nc.psum_tensor(f"sums{i}", [P, 512], fp32)) for i in range(NSUM)]
        tb = [ctx.enter_context(nc.psum_tensor(f"tb{i}", [P, 512], fp32)) for i in range(T_BANKS)]
        att = ctx.enter_context(nc.psum_tensor("att", [P, 512], fp32))
        end_banks = [tb[0], tb[1], att, tb[0]]
        v_banks = [*sums, att, *tb]

        adj_in = [sem(f"adj_in{i}") for i in range(ADJ_SLOTS)]
        wa_in, u_in, out_stored = sem("wa_in"), sem("u_in"), sem("out_stored")
        v_in = [sem(f"v_in{i}") for i in range(PARTS)]
        x_in = [sem(f"x_in{i}") for i in range(PARTS)]
        u_zero = sem("u_zero")
        consts = sem("consts")
        wa_product = sem("wa_product")
        wa_summed = sem("wa_summed")
        wa_repeated = sem("wa_repeated")
        wa1_made = sem("wa1_made")
        wa1_copied = sem("wa1_copied")
        u_turned = sem("u_turned")
        u_copied = sem("u_copied")
        v_turned = sem("v_turned")
        v_copied = sem("v_copied")
        t_made = sem("t_made")
        t_copied = sem("t_copied")
        t_low_done = sem("t_low_done")
        sum1_done = sem("sum1_done")
        mean1_done = sem("mean1_done")
        centred = sem("centred")
        squared = sem("squared")
        squares_summed = sem("squares_summed")
        var1_done = sem("var1_done")
        rstd1_done = sem("rstd1_done")
        h1_done = sem("h1_done")
        h1_weighted = sem("h1_weighted")
        s_summed = sem("s_summed")
        s_done = sem("s_done")
        mask_done = sem("mask_done")
        leaky_done = sem("leaky_done")
        w_done = sem("w_done")
        bias_done = sem("bias_done")
        exp_w = sem("exp_w")
        transposed = sem("transposed")
        weights = sem("weights")
        weights_hi = sem("weights_hi")
        weights_lo = sem("weights_lo")
        v16_made = sem("v16_made")
        att_copied = sem("att_copied")
        attended = sem("attended")
        rden_done = sem("rden_done")
        hp_done = sem("hp_done")
        low_done = sem("low_done")
        pos_done = sem("pos_done")
        exp_done = sem("exp_done")
        elu_done = sem("elu_done")
        x1_done = sem("x1_done")
        x1_kept = sem("x1_kept")
        stats_done = sem("stats_done")
        mv_done = sem("mv_done")
        eps_done = sem("eps_done")
        rstd_done = sem("rstd_done")
        norm_done = sem("norm_done")
        relu_done = sem("relu_done")
        hi_done = sem("hi_done")
        lo_done = sem("lo_done")
        gathered = sem("gathered")
        bank_done = sem("bank_done")
        rdeg_done = sem("rdeg_done")
        agg_done = sem("agg_done")
        agg_turned = sem("agg_turned")
        aggt_copied = sem("aggt_copied")
        product_done = sem("product_done")
        fin_done = sem("fin_done")

        block = ctx.enter_context(nc.Block())

        def run_steps(engine, step):
            for k in range(BODY):
                step(k, k, 0)
            with engine.Fori(0, LOOPS) as it:
                for u in range(UNROLL):
                    step(it * UNROLL + (BODY + u), BODY + u, it)
            for k in range(BODY + LOOPS * UNROLL, NB + GATHER):
                step(k, k, 0)

        def wait_all(engine, ready, *pairs):
            for _, value in pairs:
                if not isinstance(value, int):
                    engine.compute_val(value)
            engine.wait_ge(*ready)
            for semaphore, value in pairs:
                engine.wait_ge(semaphore, value)

        def live(s, lag):
            return lag <= s < NB + lag

        def at(tensor, q):
            return tensor[:, bass.ds(q, 1), :].rearrange("p o d -> p (o d)")

        @block.sync
        def _(sp):
            sp.dma_start(w_sb[:, :], W[:, :]).then_inc(wa_in, 16)
            for i in range(PARTS):
                rows = slice(i * PB, (i + 1) * PB)
                sp.dma_start(x_sb[:, rows, :], x_view[:, rows, :]).then_inc(x_in[i], 16)
            sp.wait_ge(u_zero, 1)
            for h in range(2):
                sp.dma_start(u_sb[h * D:(h + 1) * D, h * D:(h + 1) * D], U[:, :]).then_inc(u_in, 16)
            for i in range(PARTS):
                rows = slice(i * PB, (i + 1) * PB)
                sp.wait_ge(fin_done, i + 1)
                sp.dma_start(out_view[:, rows, :], fin[:, rows, :]).then_inc(out_stored, 16)
            sp.wait_ge(out_stored, 16 * PARTS)

        @block.gpsimd
        def _(pool):
            def load(k, s):
                if s >= ADJ_SLOTS:
                    pool.wait_ge(gathered, k - (ADJ_SLOTS - 1))
                pool.dma_start(adj_ring[s % ADJ_SLOTS][:, :],
                               adj_blocks[:, bass.ds(k, 1), :].rearrange("p o m -> p (o m)"))\
                    .then_inc(adj_in[s % ADJ_SLOTS], 16)

            nc.gpsimd.memset(ident[:, :], 0.0).then_inc(consts, 1)
            pool.wait_ge(consts, 1)
            nc.gpsimd.affine_select(out=ident[:, :], in_=ident[:, :], compare_op=ALU.not_equal, fill=1.0,
                                    base=0, pattern=[[-1, P]], channel_multiplier=1).then_inc(consts, 1)
            nc.gpsimd.memset(u_sb[:, :], 0.0).then_inc(u_zero, 1)
            nc.gpsimd.memset(ve[:, :, D:E], 1.0).then_inc(consts, 1)
            nc.gpsimd.memset(h2hi[:, :, D:E], H2SCALE).then_inc(consts, 1)
            nc.gpsimd.memset(minus_half[:, :], -0.5).then_inc(consts, 1)
            nc.gpsimd.memset(wscale_ln[:, :], WSCALE_LN).then_inc(consts, 1)
            nc.gpsimd.memset(v16[:, :, :, D:E], 1.0).then_inc(consts, 1)
            pool.wait_ge(consts, CONSTS)

            def wait(*pairs):
                wait_all(pool, (consts, CONSTS), *pairs)

            for i in range(PARTS + 1):
                part = slice(i * PB, (i + 1) * PB)
                if i < PARTS:
                    pool.wait_ge(var1_done, i + 1)
                    nc.gpsimd.tensor_tensor(rstd1[:, part], var1[:, part], minus_half[:, :], ALU.pow).then_inc(rstd1_done, 1)
                if i < AHEAD:
                    load(i, i)
                if i >= 1:
                    before = slice((i - 1) * PB, i * PB)
                    pool.wait_ge(wa1_copied, 1)
                    pool.wait_ge(h1_done, i)
                    nc.gpsimd.tensor_tensor(work[:, before, :], h1[:, before, :],
                                            wa1_row[:, :].unsqueeze(1).to_broadcast([P, PB, D]), ALU.mult)\
                        .then_inc(h1_weighted, 1)

            for i in range(PARTS):
                pool.wait_ge(v_in[i], 16)
            nc.gpsimd.tensor_copy(v16[:, :, :, v16_parts[0]], v_split).then_inc(v16_made, 1)
            pool.wait_ge(v16_made, 1)
            nc.gpsimd.tensor_tensor(v_rest, v_split, v16[:, :, :, v16_parts[0]], ALU.subtract).then_inc(v16_made, 1)
            pool.wait_ge(v16_made, 2)
            nc.gpsimd.tensor_copy(v16[:, :, :, v16_parts[1]], v_rest).then_inc(v16_made, 1)
            pool.wait_ge(v16_made, 3)
            nc.gpsimd.tensor_tensor(v16[:, :, :, v16_parts[2]], v_rest, v16[:, :, :, v16_parts[1]], ALU.subtract)\
                .then_inc(v16_made, 1)

            def split_rest(q, s, i):
                g = i // NS * HG + i % NS
                wait((weights, q * NG + (g + 1)), (weights_hi, q * (HALVES * NS) + (i + 1)))
                nc.gpsimd.tensor_tensor(pt_lo[:, g % HG, :], pt[:, g % PT_SLOTS, :], pt_hi[:, g % HG, :],
                                        ALU.subtract).then_inc(weights_lo, 1)

            def elu_sides(q, s):
                wait((hp_done, q + 1), *[(exp_done, q)] * (s >= 1))
                nc.gpsimd.tensor_scalar(hp_low[:, :], hp[:, :], 0.0, None, ALU.min).then_inc(low_done, 1)
                wait(*[(elu_done, q)] * (s >= 1))
                nc.gpsimd.tensor_scalar(hp_pos[:, :], hp[:, :], 0.0, -1.0, ALU.max, ALU.add).then_inc(pos_done, 1)

            def residual(q, s):
                wait((exp_done, q + 1), (pos_done, q + 1), *[(x1_done, q)] * (s >= 1))
                nc.gpsimd.tensor_tensor(elu[:, :], hp_exp[:, :], hp_pos[:, :], ALU.add).then_inc(elu_done, 1)
                wait((elu_done, q + 1), *[(x1_kept, q), (norm_done, q)] * (s >= 1))
                nc.gpsimd.tensor_tensor(x1_now[:, :], elu[:, :], at(x_sb, q), ALU.add).then_inc(x1_done, 1)
                wait((x1_done, q + 1))
                nc.gpsimd.tensor_copy(at(x1, q), x1_now[:, :]).then_inc(x1_kept, 1)

            def spread(q, s):
                wait((mv_done, q + 1))
                nc.gpsimd.tensor_scalar(var_eps[:, :], mv[:, 1:2], EPS, H2SCALE ** -2, ALU.add, ALU.mult).then_inc(eps_done, 1)
                wait((eps_done, q + 1), *[(relu_done, q)] * (s >= 1))
                nc.gpsimd.tensor_tensor(rstd2[:, :], var_eps[:, :], minus_half[:, 0:1], ALU.pow).then_inc(rstd_done, 1)
                nc.gpsimd.tensor_scalar(h2c[:, :], x1_now[:, :], mv[:, 0:1], None, ALU.subtract).then_inc(norm_done, 1)

            def h2_rest(q, s):
                wait((hi_done, q + 1))
                nc.gpsimd.tensor_tensor(h2lo[:, s % 2, :], h2s[:, :], h2hi[:, s % 2, 0:D], ALU.subtract)\
                    .then_inc(lo_done, 1)

            def step(k, s, turn):
                q, sq = k - CLOSE, s - CLOSE
                if live(s, 2):
                    split_rest(k - 2, s - 2, 0)
                if live(s, CLOSE + 1):
                    h2_rest(q - 1, sq - 1)
                if live(s, 2):
                    split_rest(k - 2, s - 2, 1)
                if live(s, CLOSE):
                    elu_sides(q, sq)
                    residual(q, sq)
                if live(s, 2):
                    split_rest(k - 2, s - 2, 2)
                    split_rest(k - 2, s - 2, 3)
                if live(s, CLOSE):
                    spread(q, sq)
                if s + AHEAD < NB:
                    load(k + AHEAD, s + AHEAD)

            run_steps(pool, step)

        @block.scalar
        def _(act):
            act.dma_start(a_all[:, :, :].rearrange("p h d -> p (h d)"), a.rearrange("m o -> (m o)").partition_broadcast(D))\
                .then_inc(wa_in, 16)
            for i in range(PARTS):
                chunks = slice(i * NC // PARTS, (i + 1) * NC // PARTS)
                act.dma_start(ve[:, chunks, 0:D], v_view[:, chunks, :]).then_inc(v_in[i], 16)
            act.wait_ge(wa_summed, 1)
            for h in range(2):
                nc.scalar.activation(wa_rep[:, h, :], wa_sb[:, h:h + 1].to_broadcast([D, P]), ACT.Copy)\
                    .then_inc(wa_repeated, 1)
            act.wait_ge(wa1_made, 1)
            nc.scalar.activation(wa1_row[:, :], tb[1][:, 0:D], ACT.Copy).then_inc(wa1_copied, 1)

            def square(i):
                act.wait_ge(centred, i + 1)
                part = slice(i * PB, (i + 1) * PB)
                nc.scalar.activation(work[:, part, :], h1[:, part, :], ACT.Square).then_inc(squared, 1)

            for i in range(PARTS - 1):
                square(i)
            for g in range(NG):
                act.wait_ge(v_turned, g + 1)
                nc.scalar.activation(vt[:, g, :], v_banks[g][0:D, :], ACT.Copy).then_inc(v_copied, 1)
                if g == 2:
                    square(PARTS - 1)
            for g in range(NG):
                act.wait_ge(t_made, g + 1)
                nc.scalar.activation(t_row[:, g * 512:(g + 1) * 512], v_banks[g][:, :], ACT.Copy, scale=-1.0)\
                    .then_inc(t_copied, 1)
            act.wait_ge(u_turned, 1)
            nc.scalar.activation(ut[:, :], tb[1][:, 2 * P:3 * P], ACT.Copy).then_inc(u_copied, 1)

            def make_bias(q, s):
                act.wait_ge(consts, CONSTS)
                act.wait_ge(w_done, q + 1)
                if s >= 2:
                    act.wait_ge(exp_w, 4 * (q - 1))
                nc.scalar.activation(bias[:, s % 2:s % 2 + 1], w_min[:, s % 2:s % 2 + 1], ACT.Identity,
                                     bias=wscale_ln[:, 0:1]).then_inc(bias_done, 1)

            def exponentials(q, s, part):
                quarter = w[s % W_SLOTS][:, part * QUARTER:(part + 1) * QUARTER]
                act.wait_ge(w_done, q + 1)
                act.wait_ge(bias_done, q + 1)
                nc.scalar.activation(quarter, quarter, ACT.Exp, bias=bias[:, s % 2:s % 2 + 1], scale=-1.0).then_inc(exp_w, 1)

            def evacuate(q, s, g):
                act.wait_ge(transposed, q * NG + (g + 1))
                if s >= 1 or g >= HG:
                    act.wait_ge(attended, q * NG + (g + 1 - HG))
                if g % HG in SPLIT:
                    nc.scalar.activation(pt_hi[:, g % HG, :], tb[g % T_BANKS][:, :], ACT.Copy).then_inc(weights_hi, 1)
                nc.scalar.activation(pt[:, g % PT_SLOTS, :], tb[g % T_BANKS][:, :], ACT.Copy).then_inc(weights, 1)

            def copy_att(q, s):
                act.wait_ge(attended, q * NG + NG)
                if s >= 2:
                    act.wait_ge(hp_done, q - 1)
                nc.scalar.activation(att_sb[:, s % 2, :], att[:, 0:E], ACT.Copy).then_inc(att_copied, 1)

            def elu_exp(q, s):
                act.wait_ge(low_done, q + 1)
                if s >= 1:
                    act.wait_ge(elu_done, q)
                nc.scalar.activation(hp_exp[:, :], hp_low[:, :], ACT.Exp).then_inc(exp_done, 1)

            def h2_whole(q, s):
                act.wait_ge(rstd_done, q + 1)
                act.wait_ge(norm_done, q + 1)
                if s >= 1:
                    act.wait_ge(lo_done, q)
                nc.scalar.activation(h2s[:, :], h2c[:, :], ACT.Relu, scale=rstd2[:, 0:1]).then_inc(relu_done, 1)

            def h2_high(q, s):
                act.wait_ge(relu_done, q + 1)
                if s >= 2:
                    act.wait_ge(gathered, q - 1)
                nc.scalar.activation(h2hi[:, s % 2, 0:D], h2s[:, :], ACT.Copy).then_inc(hi_done, 1)

            def step(k, s, turn):
                for g in range(NG):
                    if live(s, CLOSE) and g == ATT_AT:
                        copy_att(k - CLOSE, s - CLOSE)
                    if live(s, 2):
                        evacuate(k - 2, s - 2, g)
                    if live(s, CLOSE + 1) and g == RELU_AT:
                        h2_whole(k - CLOSE - 1, s - CLOSE - 1)
                    if live(s, 1) and g == RELU_AT:
                        make_bias(k - 1, s - 1)
                    if live(s, CLOSE + 1) and g == RELU_AT:
                        h2_high(k - CLOSE - 1, s - CLOSE - 1)
                    if live(s, CLOSE) and g == ELU_AT:
                        elu_exp(k - CLOSE, s - CLOSE)
                    if live(s, 1) and g in EXP_AT:
                        exponentials(k - 1, s - 1, EXP_AT.index(g))

            run_steps(act, step)

            for g in range(PARTS):
                act.wait_ge(agg_turned, g + 1)
                nc.scalar.activation(aggt[:, g, :], end_banks[g][:, :], ACT.Copy).then_inc(aggt_copied, 1)

        @block.vector
        def _(dve):
            dve.wait_ge(wa_in, 32)
            nc.vector.tensor_tensor(w_times_a[:, :, :], a_all[:, :, :], w_sb[:, :].unsqueeze(1).to_broadcast([D, 2, D]),
                                    ALU.mult).then_inc(wa_product, 1)
            dve.wait_ge(wa_product, 1)
            nc.vector.tensor_reduce(wa_sb[:, :], w_times_a[:, :, :], AX.X, ALU.add).then_inc(wa_summed, 1)

            def part_of(i):
                part = slice(i * PB, (i + 1) * PB)
                return (x_sb[:, part, :], h1[:, part, :], work[:, part, :], mean1[:, part], var1[:, part], tmp1[:, part],
                        rstd1[:, part], s_high[:, part])

            def wide(col):
                return col.unsqueeze(2).to_broadcast([P, PB, D])

            def centre(i):
                xp, hh, _, mean, *_ = part_of(i)
                dve.wait_ge(x_in[i], 16)
                nc.vector.tensor_reduce(mean, xp, AX.X, ALU.add).then_inc(sum1_done, 1)
                dve.wait_ge(sum1_done, i + 1)
                nc.vector.tensor_scalar(mean, mean, 1.0 / D, None, ALU.mult).then_inc(mean1_done, 1)
                dve.wait_ge(mean1_done, i + 1)
                nc.vector.tensor_tensor(hh, xp, wide(mean), ALU.subtract).then_inc(centred, 1)

            def variance(i):
                _, _, ww, _, var, tmp, *_ = part_of(i)
                dve.wait_ge(squared, i + 1)
                nc.vector.tensor_reduce(tmp, ww, AX.X, ALU.add).then_inc(squares_summed, 1)
                dve.wait_ge(squares_summed, i + 1)
                nc.vector.tensor_scalar(var, tmp, 1.0 / D, EPS, ALU.mult, ALU.add).then_inc(var1_done, 1)

            def scale(i):
                _, hh, _, _, _, _, rstd, _ = part_of(i)
                dve.wait_ge(rstd1_done, i + 1)
                nc.vector.scalar_tensor_tensor(out=hh, in0=hh, scalar=0.0, in1=wide(rstd), op0=ALU.max, op1=ALU.mult)\
                    .then_inc(h1_done, 1)

            def row_scores(i):
                _, _, ww, _, _, tmp, _, s_part = part_of(i)
                dve.wait_ge(h1_weighted, i + 1)
                nc.vector.tensor_reduce(tmp, ww, AX.X, ALU.add).then_inc(s_summed, 1)
                dve.wait_ge(s_summed, i + 1)
                nc.vector.tensor_scalar(s_part, tmp, SLOPE - 1.0, None, ALU.mult).then_inc(s_done, 1)

            def scale_t(groups):
                for g in groups:
                    dve.wait_ge(t_copied, g + 1)
                    columns = slice(g * 512, (g + 1) * 512)
                    nc.vector.tensor_scalar(t_low[:, columns], t_row[:, columns], SLOPE, None, ALU.mult).then_inc(t_low_done, 1)

            for i in range(PARTS + 1):
                if i < PARTS:
                    centre(i)
                if 0 <= i - 2:
                    scale(i - 2)
                if 0 <= i - 1:
                    variance(i - 1)
                if 0 <= i - 3:
                    row_scores(i - 3)
            scale_t(range(0, 3))
            scale(PARTS - 1)
            scale_t(range(3, 5))
            row_scores(PARTS - 2)
            scale_t(range(5, 6))
            row_scores(PARTS - 1)
            scale_t(range(6, NG))
            dve.wait_ge(s_done, PARTS)

            def make_mask(k, s, turn):
                dve.wait_ge(adj_in[s % ADJ_SLOTS], turn * 16 + 16 * (s // ADJ_SLOTS + 1))
                if s >= 1:
                    dve.wait_ge(w_done, k)
                nc.vector.tensor_scalar(mask[:, :], adj_ring[s % ADJ_SLOTS][:, :], 0.0, MASKED, ALU.is_le, ALU.mult)\
                    .then_inc(mask_done, 1)

            def leaky(k, s):
                dve.wait_ge(t_low_done, NG)
                if s == 2:
                    dve.wait_ge(v16_made, 4)
                for h in range(2):
                    half = slice(h * M // 2, (h + 1) * M // 2)
                    if s >= W_SLOTS:
                        dve.wait_ge(transposed, (k - W_SLOTS) * NG + (h + 1) * NG // 2)
                    nc.vector.scalar_tensor_tensor(out=w[s % W_SLOTS][:, half], in0=t_row[:, half],
                                                   scalar=s_high[:, bass.ds(k, 1)], in1=t_low[:, half],
                                                   op0=ALU.add, op1=ALU.min).then_inc(leaky_done, 1)

            def add_mask(k, s):
                wait_all(dve, (t_copied, NG), (mask_done, k + 1), (leaky_done, 2 * k + 2), *[(bias_done, k - 1)] * (s >= 2))
                nc.vector.tensor_tensor_reduce(
                    out=w[s % W_SLOTS][:, :], in0=mask[:, :], in1=w[s % W_SLOTS][:, :], scale=1.0,
                    scalar=3.0e38, op0=ALU.add, op1=ALU.min, accum_out=w_min[:, s % 2:s % 2 + 1]).then_inc(w_done, 1)

            def invert(q, s):
                dve.wait_ge(att_copied, q + 1)
                nc.vector.reciprocal(rden[:, :], att_sb[:, s % 2, D:E]).then_inc(rden_done, 1)

            def divide(q, s):
                dve.wait_ge(rden_done, q + 1)
                if s >= 1:
                    dve.wait_ge(pos_done, q)
                nc.vector.scalar_tensor_tensor(out=hp[:, :], in0=att_sb[:, s % 2, 0:D], scalar=rden[:, 0:1],
                                               in1=at(h1, q), op0=ALU.mult, op1=ALU.add).then_inc(hp_done, 1)

            def statistics(q, s):
                dve.wait_ge(x1_done, q + 1)
                if s >= 1:
                    dve.wait_ge(mv_done, q)
                nc.vector.bn_stats(stats[:, :], x1_now[:, :]).then_inc(stats_done, 1)

            def aggregate(q, s):
                wait_all(dve, (t_copied, NG), (stats_done, q + 1), *[(norm_done, q)] * (s >= 1))
                nc.vector.bn_aggr(mv[:, :], stats[:, :]).then_inc(mv_done, 1)

            def step(k, s, turn):
                if live(s, 0):
                    make_mask(k, s, turn)
                if live(s, CLOSE + 1):
                    aggregate(k - CLOSE - 1, s - CLOSE - 1)
                if live(s, 0):
                    leaky(k, s)
                if live(s, CLOSE):
                    invert(k - CLOSE, s - CLOSE)
                    divide(k - CLOSE, s - CLOSE)
                if live(s, 0):
                    add_mask(k, s)
                if live(s, CLOSE):
                    statistics(k - CLOSE, s - CLOSE)

            run_steps(dve, step)

            for b in range(NSUM):
                if b < NSUM - 1:
                    dve.wait_ge(bank_done, b + 1)
                else:
                    dve.wait_ge(gathered, NB)
                c0, m = b * CB, min(CB, NB - b * CB)
                bank = sums[b][:, 0:m * E].rearrange("p (c e) -> p c e", e=E)
                nc.vector.reciprocal(rdeg[:, c0:c0 + m], bank[:, :, D:E].rearrange("p c o -> p (c o)"))\
                    .then_inc(rdeg_done, 1)
                dve.wait_ge(rdeg_done, b + 1)
                nc.vector.tensor_tensor(agg[:, c0:c0 + m, :], bank[:, :, 0:D],
                                        rdeg[:, c0:c0 + m].unsqueeze(2).to_broadcast([P, m, D]), ALU.mult)\
                    .then_inc(agg_done, 1)
            dve.wait_ge(x1_kept, NB)
            for g in range(PARTS):
                rows = slice(g * PB, (g + 1) * PB)
                dve.wait_ge(product_done, g + 1)
                nc.vector.scalar_tensor_tensor(out=fin[:, rows, :], in0=sums[g][:, :].rearrange("p (c d) -> p c d", d=D),
                                               scalar=0.0, in1=x1[:, rows, :], op0=ALU.max, op1=ALU.add)\
                    .then_inc(fin_done, 1)

        @block.tensor
        def _(pe):
            def turn_over(out_ap, in_ap, rows=P):
                return nc.tensor.transpose(out_ap, in_ap, ident[0:rows, 0:rows])

            pe.wait_ge(consts, 2)
            pe.wait_ge(wa_repeated, 2)
            nc.tensor.matmul(tb[1][:, 0:D], wa_rep[:, 0, :], ident[0:D, 0:D], start=True, stop=True).then_inc(wa1_made, 1)
            for i in range(PARTS - 1):
                pe.wait_ge(v_in[i], 16)
            for g in range(NG):
                if g == NG - NG // PARTS:
                    pe.wait_ge(v_in[PARTS - 1], 16)
                if v_banks[g] is tb[1]:
                    pe.wait_ge(wa1_copied, 1)
                for i in range(G):
                    last = turn_over(v_banks[g][0:D, i * P:(i + 1) * P], ve[:, g * G + i, 0:D])
                last.then_inc(v_turned, 1)
            for g in range(NG):
                pe.wait_ge(v_copied, g + 1)
                nc.tensor.matmul(v_banks[g][:, :], wa_rep[:, 1, :], vt[:, g, :], start=True, stop=True).then_inc(t_made, 1)
            pe.wait_ge(u_in, 32)
            pe.wait_ge(t_copied, NG)
            turn_over(tb[1][:, 2 * P:3 * P], u_sb[:, :]).then_inc(u_turned, 1)
            pe.wait_ge(u_copied, 1)
            pe.wait_ge(consts, CONSTS)
            pe.wait_ge(v16_made, 4)

            def transposes(q, s, g):
                pe.wait_ge(exp_w, 4 * q + (g // 2 + 1))
                if s > 0 or g >= T_BANKS:
                    pe.wait_ge(weights, q * NG + (g + 1 - T_BANKS))
                for i in range(G):
                    c = g * G + i
                    last = turn_over(tb[g % T_BANKS][:, i * P:(i + 1) * P], w[s % W_SLOTS][:, c * P:(c + 1) * P])
                last.then_inc(transposed, 1)

            def attend(q, s, g):
                if g % HG in SPLIT:
                    pe.wait_ge(weights_lo, q * (HALVES * NS) + (g // HG * NS + g % HG + 1))
                    pe.wait_ge(weights_hi, q * (HALVES * NS) + (g // HG * NS + g % HG + 1))
                else:
                    pe.wait_ge(weights, q * NG + (g + 1))
                if g == 0 and s >= 1:
                    pe.wait_ge(att_copied, q)
                for i in range(G):
                    c = g * G + i
                    if g % HG in SPLIT:
                        high, low = (part[:, g % HG, i * P:(i + 1) * P] for part in (pt_hi, pt_lo))
                        v0, v1, v2 = (v16[:, c // (HG * G), c % (HG * G), part]
                                      for part in (slice(0, E), *v16_parts[1:]))
                        nc.tensor.matmul(att[:, 0:E], high, v0, start=(c == 0), stop=False)
                        nc.tensor.matmul(att[:, 0:D], high, v1, start=False, stop=False)
                        nc.tensor.matmul(att[:, 0:D], high, v2, start=False, stop=False)
                        nc.tensor.matmul(att[:, 0:E], low, v0, start=False, stop=False)
                        last = nc.tensor.matmul(att[:, 0:D], low, v1, start=False, stop=False)
                        continue
                    last = nc.tensor.matmul(att[:, 0:E], pt[:, g % PT_SLOTS, i * P:(i + 1) * P], ve[:, c, :],
                                            start=(c == 0), stop=(c == NC - 1))
                last.then_inc(attended, 1)

            def gather(q, s, chunks):
                if chunks[0] == 0:
                    pe.wait_ge(lo_done, q + 1)
                    pe.wait_ge(hi_done, q + 1)
                for c in chunks:
                    columns = adj_ring[s % ADJ_SLOTS][:, c * P:(c + 1) * P]
                    bank, at0 = sums[c // CB], (c % CB) * E
                    nc.tensor.matmul(bank[:, at0:at0 + E], columns, h2hi[:, s % 2, :],
                                     start=(s == 0 and c % CB == 0), stop=False, skip_group_check=True)
                    last = nc.tensor.matmul(bank[:, at0:at0 + D], columns, h2lo[:, s % 2, :],
                                            start=False, stop=(s == NB - 1), skip_group_check=True)
                    if s == NB - 1 and (c % CB == CB - 1) and c < NC - 1:
                        last.then_inc(bank_done, 1)
                if chunks[-1] == NC - 1:
                    last.then_inc(gathered, 1)

            def step(k, s, turn):
                for g in range(NG):
                    if live(s, 2):
                        transposes(k - 2, s - 2, g)
                    if live(s, GATHER):
                        for chunks in GATHER_AT[g]:
                            gather(k - GATHER, s - GATHER, range(chunks * G, chunks * G + G))
                    if g < LAG and live(s, 3):
                        attend(k - 3, s - 3, g + NG - LAG)
                    if g >= LAG and live(s, 2):
                        attend(k - 2, s - 2, g - LAG)

            run_steps(pe, step)

            def product(g):
                pe.wait_ge(aggt_copied, g + 1)
                for i in range(G):
                    pair = slice(i * P, (i + 1) * P)
                    last = nc.tensor.matmul(sums[g][:, pair], aggt[:, g, pair], ut[:, :], start=True, stop=True)
                last.then_inc(product_done, 1)

            for g in range(PARTS):
                pe.wait_ge(agg_done, ((g + 1) * PB - 1) // CB + 1)
                if g == PARTS - 1:
                    product(0)
                for i in range(G):
                    b = g * PB + 2 * i
                    last = turn_over(end_banks[g][:, i * P:(i + 1) * P], agg[:, b:b + 2, :].rearrange("p b d -> p (b d)"))
                last.then_inc(agg_turned, 1)
            for g in range(1, PARTS):
                product(g)


_INS = ['x', 'adj', 'L0_gnn_entity_embs', 'L0_gnn_W', 'L0_gnn_a', 'L1_gnn_U']
_OUTS = [((4096, 64), 'float32')]


def kernel(**inputs):
    import numpy as _np
    import concourse.bacc as _bacc
    from concourse import mybir as _mybir
    from concourse.bass_utils import run_bass_kernel_spmd as _run

    nc = _bacc.Bacc("TRN2", target_bir_lowering=False, num_devices=1)
    arrays, args = {}, []
    for name in _INS:
        a = _np.ascontiguousarray(inputs[name])
        arrays[f"in_{name}_dram"] = a
        args.append(nc.dram_tensor(f"in_{name}_dram", a.shape, _mybir.dt.from_np(a.dtype), kind="ExternalInput").ap())
    for i, (shape, dtype) in enumerate(_OUTS):
        dt = _mybir.dt.from_np(_np.dtype(dtype))
        args.append(nc.dram_tensor(f"out_{i}_dram", shape, dt, kind="ExternalOutput").ap())
    graph_layers_kernel(nc, *args)
    r = _run(nc, [arrays], core_ids=[0])
    return r.results[0]["out_0_dram"]
```
